# Optimizing a Trainium2 kernel written in Bass

```python
import numpy as np
import jax
import jax.numpy as jnp

def _softmax(x, axis=-1):
    return jax.nn.softmax(x, axis=axis)

def _gelu(x):
    return jax.nn.gelu(x, approximate=True)

def _silu(x):
    return jax.nn.silu(x)

def _sigmoid(x):
    return jax.nn.sigmoid(x)

def _layernorm(x, axis=-1, eps=1e-05):
    m = jnp.mean(x, axis=axis, keepdims=True)
    v = jnp.var(x, axis=axis, keepdims=True)
    return (x - m) / jnp.sqrt(v + eps)

def _scatter_add(tgt, idx, src, axis=0):
    return tgt.at[idx].add(src)

def _segment_sum(src, seg, n):
    return jax.ops.segment_sum(src, seg, n)
kernel_name = 'mk_gnn_ffn_d1_gnn_r32_6f23ae'

def setup_inputs(seed: int=0):
    np.random.seed(seed)
    _w = jnp.asarray

    def _rec_inputs():
        import jax
        import jax.numpy as jnp
        _gk = jax.random.key(seed)
        x = -0.0002117 + 1 * jax.random.normal(jax.random.fold_in(_gk, 1), (3125, 256), jnp.float32)
        src = jax.random.randint(jax.random.fold_in(_gk, 2), (50000,), 0, 3125, jnp.int32)
        dst = jax.random.randint(jax.random.fold_in(_gk, 3), (50000,), 0, 3125, jnp.int32)
        _o = jnp.argsort(dst, stable=True)
        src = src[_o]
        dst = dst[_o]
        edge_weight = 0.000714719 + 1.00021 * jax.random.normal(jax.random.fold_in(_gk, 12), (50000,), jnp.float32)
        return (x, src, dst, edge_weight)
    x, src, dst, edge_weight = _rec_inputs()

    def _L0_gnn_setup():
        import jax, jax.numpy as jnp
        import numpy as np
        N = 3125
        E = 100000
        D = 256
        LN_EPS = 1e-05

        def _safe(x):
            return jnp.nan_to_num(x, nan=0.0, posinf=0.0, neginf=0.0)

        def _layernorm(h, g, b):
            mu = jnp.mean(h, axis=-1, keepdims=True)
            var = jnp.mean(jnp.square(h - mu), axis=-1, keepdims=True)
            return (h - mu) * jax.lax.rsqrt(var + LN_EPS) * g + b

        def _gcn_conv(h, row, col, ew, dis, W, b):
            xw = h @ W
            norm = dis[row] * ew * dis[col]
            msg = norm[:, None] * xw[row]
            agg = jax.ops.segment_sum(msg, col, num_segments=N)
            agg = agg + (dis * dis)[:, None] * xw
            return agg + b
        key = jax.random.key(seed)
        ks = jax.random.split(key, 8)
        x = jax.random.normal(ks[0], (N, D), dtype=jnp.float32)
        edge_index = jax.random.randint(ks[1], (2, E), 0, N, dtype=jnp.int64)
        edge_weight = jax.random.normal(ks[2], (E,), dtype=jnp.float32)
        s = 1.0 / np.sqrt(D)
        W1 = jax.random.uniform(ks[3], (D, D), jnp.float32, -s, s)
        W2 = jax.random.uniform(ks[4], (D, D), jnp.float32, -s, s)
        b1 = jax.random.uniform(ks[5], (D,), jnp.float32, -s, s)
        b2 = jax.random.uniform(ks[6], (D,), jnp.float32, -s, s)
        ln_g1 = jnp.ones((D,), jnp.float32)
        ln_b1 = jnp.zeros((D,), jnp.float32)
        ln_g2 = jnp.ones((D,), jnp.float32)
        ln_b2 = jnp.zeros((D,), jnp.float32)
        return dict(x=x, edge_index=edge_index, edge_weight=edge_weight, W1=W1, b1=b1, ln_g1=ln_g1, ln_b1=ln_b1, W2=W2, b2=b2, ln_g2=ln_g2, ln_b2=ln_b2)
    _L0_gnn_all = _L0_gnn_setup()
    _L0_gnn_in = {k: v for k, v in _L0_gnn_all.items() if k in ('W1', 'b1', 'ln_g1', 'ln_b1', 'W2', 'b2', 'ln_g2', 'ln_b2')}
    del _L0_gnn_all

    def _L0_ffn_setup():
        import jax, jax.numpy as jnp
        import numpy as np
        B, S, H, F, E, K = (8, 128, 256, 512, 16, 2)
        EPS = 1e-05
        key = jax.random.key(seed)
        ks = jax.random.split(key, 9)
        sc = 0.02
        return {'x': jax.random.normal(ks[0], (B, S, H), dtype=jnp.float32), 'gate_w': jax.random.normal(ks[1], (H, E), dtype=jnp.float32) * sc, 'gate_b': jnp.zeros((E,), dtype=jnp.float32), 'w1': jax.random.normal(ks[2], (E, H, F), dtype=jnp.float32) * sc, 'b1': jnp.zeros((E, F), dtype=jnp.float32), 'w2': jax.random.normal(ks[3], (E, F, H), dtype=jnp.float32) * sc, 'b2': jnp.zeros((E, H), dtype=jnp.float32), 'gamma': jnp.ones((H,), dtype=jnp.float32), 'beta': jnp.zeros((H,), dtype=jnp.float32)}
    _L0_ffn_all = _L0_ffn_setup()
    _L0_ffn_in = {k: v for k, v in _L0_ffn_all.items() if k in ('gate_w', 'gate_b', 'w1', 'b1', 'w2', 'b2', 'gamma', 'beta')}
    del _L0_ffn_all
    return {'x': x, 'src': src, 'dst': dst, 'edge_weight': edge_weight, 'L0_gnn_W1': _L0_gnn_in['W1'], 'L0_gnn_b1': _L0_gnn_in['b1'], 'L0_gnn_ln_g1': _L0_gnn_in['ln_g1'], 'L0_gnn_ln_b1': _L0_gnn_in['ln_b1'], 'L0_gnn_W2': _L0_gnn_in['W2'], 'L0_gnn_b2': _L0_gnn_in['b2'], 'L0_gnn_ln_g2': _L0_gnn_in['ln_g2'], 'L0_gnn_ln_b2': _L0_gnn_in['ln_b2'], 'L0_ffn_gate_w': _L0_ffn_in['gate_w'], 'L0_ffn_gate_b': _L0_ffn_in['gate_b'], 'L0_ffn_w1': _L0_ffn_in['w1'], 'L0_ffn_b1': _L0_ffn_in['b1'], 'L0_ffn_w2': _L0_ffn_in['w2'], 'L0_ffn_b2': _L0_ffn_in['b2'], 'L0_ffn_gamma': _L0_ffn_in['gamma'], 'L0_ffn_beta': _L0_ffn_in['beta']}

def reference(x, src, dst, edge_weight, L0_gnn_W1, L0_gnn_b1, L0_gnn_ln_g1, L0_gnn_ln_b1, L0_gnn_W2, L0_gnn_b2, L0_gnn_ln_g2, L0_gnn_ln_b2, L0_ffn_gate_w, L0_ffn_gate_b, L0_ffn_w1, L0_ffn_b1, L0_ffn_w2, L0_ffn_b2, L0_ffn_gamma, L0_ffn_beta):
    import jax
    import jax.numpy as jnp

    def _L0_gnn_ref(x, edge_index, edge_weight, W1, b1, ln_g1, ln_b1, W2, b2, ln_g2, ln_b2):
        import jax, jax.numpy as jnp
        import numpy as np
        N = 3125
        E = 100000
        D = 256
        LN_EPS = 1e-05

        def _safe(x):
            return jnp.nan_to_num(x, nan=0.0, posinf=0.0, neginf=0.0)

        def _layernorm(h, g, b):
            mu = jnp.mean(h, axis=-1, keepdims=True)
            var = jnp.mean(jnp.square(h - mu), axis=-1, keepdims=True)
            return (h - mu) * jax.lax.rsqrt(var + LN_EPS) * g + b

        def _gcn_conv(h, row, col, ew, dis, W, b):
            xw = h @ W
            norm = dis[row] * ew * dis[col]
            msg = norm[:, None] * xw[row]
            agg = jax.ops.segment_sum(msg, col, num_segments=N)
            agg = agg + (dis * dis)[:, None] * xw
            return agg + b
        row, col = (edge_index[0], edge_index[1])
        h = _safe(x)
        ew = jnp.clip(jnp.abs(_safe(edge_weight.reshape(-1))), 1e-06, None)
        deg = jax.ops.segment_sum(ew, col, num_segments=N) + 1.0
        dis = jax.lax.rsqrt(deg)
        for W, b, g, be in ((W1, b1, ln_g1, ln_b1), (W2, b2, ln_g2, ln_b2)):
            h_res = h
            h = _gcn_conv(h, row, col, ew, dis, W, b)
            h = _safe(h)
            h = _safe(_layernorm(h, g, be))
            h = jax.nn.relu(h)
            h = _safe(h)
            h = _safe(h + h_res)
        return h

    def _L0_ffn_ref(x, gate_w, gate_b, w1, b1, w2, b2, gamma, beta):
        import jax, jax.numpy as jnp
        import numpy as np
        B, S, H, F, E, K = (8, 128, 256, 512, 16, 2)
        EPS = 1e-05
        gate_logits = x @ gate_w + gate_b
        topk_vals, topk_idx = jax.lax.top_k(gate_logits, K)
        topk_w = jax.nn.softmax(topk_vals, axis=-1)
        h = jax.nn.relu(jnp.einsum('bsh,ehf->bsef', x, w1) + b1)
        expert_out = jnp.einsum('bsef,efh->bseh', h, w2) + b2
        sel = jnp.take_along_axis(expert_out, topk_idx[:, :, :, None], axis=2)
        moe = jnp.sum(topk_w[..., None] * sel, axis=2)
        y = x + moe
        mu = jnp.mean(y, axis=-1, keepdims=True)
        var = jnp.var(y, axis=-1, keepdims=True)
        return (y - mu) / jnp.sqrt(var + EPS) * gamma + beta
    edge_index = jnp.stack([src, dst])
    x = x + _L0_gnn_ref(_layernorm(x, axis=-1), edge_index, edge_weight, L0_gnn_W1, L0_gnn_b1, L0_gnn_ln_g1, L0_gnn_ln_b1, L0_gnn_W2, L0_gnn_b2, L0_gnn_ln_g2, L0_gnn_ln_b2)
    x = x + _L0_ffn_ref(_layernorm(x, axis=-1)[None], L0_ffn_gate_w, L0_ffn_gate_b, L0_ffn_w1, L0_ffn_b1, L0_ffn_w2, L0_ffn_b2, L0_ffn_gamma, L0_ffn_beta)[0]
    return x

_drawn_inputs = setup_inputs


def setup_inputs(seed=0):
    import zlib

    import numpy as np

    out = dict(_drawn_inputs(seed))
    spreads = {'L0_gnn_ln_g1': (1.0, 0.2),
     'L0_gnn_ln_b1': (0.0, 0.1),
     'L0_gnn_ln_g2': (1.0, 0.2),
     'L0_gnn_ln_b2': (0.0, 0.1),
     'L0_ffn_gate_b': (0.0, 0.388),
     'L0_ffn_b1': (0.0, 0.8),
     'L0_ffn_b2': (0.0, 0.356),
     'L0_ffn_gamma': (1.0, 0.2),
     'L0_ffn_beta': (0.0, 0.1)}
    factors = {'L0_ffn_w1': 3.011}
    for name, (base, spread) in spreads.items():
        noise = np.random.default_rng([zlib.crc32(name.encode()), seed]).standard_normal(out[name].shape)
        drawn = base * np.exp(spread * noise) if base else spread * noise
        out[name] = jnp.asarray(drawn.astype(out[name].dtype))
    for name, factor in factors.items():
        out[name] = (out[name] * factor).astype(out[name].dtype)
    return out
```

```python
from contextlib import ExitStack

import concourse.bass as bass
from concourse import mybir

F32 = mybir.dt.float32
BF16 = mybir.dt.bfloat16
I32 = mybir.dt.int32
U32 = mybir.dt.uint32
U16 = mybir.dt.uint16
ALU = mybir.AluOpType
ACT = mybir.ActivationFunctionType
AX_X = mybir.AxisListType.X

P = 128
N, D, E = 3125, 256, 50000
EXPERTS, F = 16, 512
EPS = 1e-5
KD, KF = D // P, F // P
NT = -(-N // P)
LAST = N - (NT - 1) * P
ET = -(-E // P)
EFULL = E // P
EREST = E - EFULL * P
EC = -(-ET // P)
GROUP = 8
RING = 2 * GROUP
STEPS = -(-(ET + NT - 1) // RING) * RING
BANKS, BANK = 8, 512
SLOTS, SLOT = BANKS, BANK
UN = 5
BLOCKS = (2 * N + EXPERTS * (P - 1)) // P
ROWS = BLOCKS * P


def program(nc, x, src, dst, edge_weight, gw1, gb1, gg1, gn1, gw2, gb2, gg2, gn2,
            gate_w, gate_b, ew1, eb1, ew2, eb2, gamma, beta, out):
    table = nc.dram_tensor("scaled_rows", (NT * P, D), F32, kind="Internal").ap()
    x1_dram = nc.dram_tensor("after_gnn", (NT * P, D), F32, kind="Internal").ap()
    rows_in = nc.dram_tensor("expert_rows_in", (ROWS, D), F32, kind="Internal").ap()
    rows_out = nc.dram_tensor("expert_rows_out", (ROWS, D), F32, kind="Internal").ap()

    with ExitStack() as outer:
        def sem(name):
            return outer.enter_context(nc.semaphore(name))

        def keep(name, shape, dt=F32):
            return outer.enter_context(nc.sbuf_tensor(name, shape, dt))

        ident = keep("ident", [P, P])
        eps = keep("eps", [P, 1])
        ones = keep("ones", [P, P], BF16)
        below = keep("below", [P, P], BF16)
        x2 = keep("x2", [P, NT, D])
        slot_id = keep("slot_id", [P, 2, NT], I32)
        top_w = keep("top_w", [P, 2, NT])
        logits = keep("logits", [P, NT, EXPERTS])
        w_off = keep("w_off", [P, BLOCKS], I32)
        ps = outer.enter_context(nc.psum_tensor("ps", [P, BANKS * BANK], F32))
        ps_slot = ps[:, :]
        ps_a, ps_b, ps_c, ps_d = (ps[:, k * BANK:(k + 1) * BANK] for k in range(4))

        zeroed_rows = sem("zeroed_rows")

        gnn(nc, sem, locals())
        with ExitStack() as ctx:
            route(nc, sem, locals(), logits,
                  lambda name, shape, dt=F32: ctx.enter_context(nc.sbuf_tensor(name, shape, dt)))
        experts(nc, sem, locals())


def gnn(nc, sem, g):
    x, src, dst, edge_weight = g["x"], g["src"], g["dst"], g["edge_weight"]
    ident, ones, below, x2 = g["ident"], g["ones"], g["below"], g["x2"]
    table, x1_dram, rows_in = g["table"], g["x1_dram"], g["rows_in"]
    ps_slot, ps_a, ps_b, ps_c, ps_d = g["ps_slot"], g["ps_a"], g["ps_b"], g["ps_c"], g["ps_d"]
    logits, eps = g["logits"], g["eps"]
    with ExitStack() as ctx:
        def sb(name, shape, dt=F32):
            return ctx.enter_context(nc.sbuf_tensor(name, shape, dt))

        h = sb("h", [P, NT, D])
        xin = sb("xin", [P, NT, D])
        scaled = sb("scaled", [P, NT, D])
        sums = sb("sums", [P, NT, D])
        rows = sb("rows", [P, RING, D])
        smat = sb("smat", [P, RING, P])
        e_int = sb("e_int", [P, 2, EC, P], I32)
        e_f = sb("e_f", [P, 3, EC, P])
        bad_e = sb("bad_e", [P, EC, P], I32)
        iota = sb("iota", [P, STEPS])
        part = sb("part", [P, EC])
        bounds = sb("bounds", [P, NT])
        before = sb("before", [P, EC, NT], BF16)
        first = sb("first", [P, 1])
        begun = sb("begun", [P, STEPS], BF16)
        node_of = sb("node_of", [P, STEPS])
        edge_of = sb("edge_of", [P, STEPS])
        pick = sb("pick", [P, EC, STEPS])
        node_i = sb("node_i", [P, STEPS], I32)
        node_next = sb("node_next", [P, STEPS], U16)
        slot_off = sb("slot_off", [P, STEPS], I32)
        ends = sb("ends", [P, 32], U16)
        ends_f = sb("ends_f", [P, NT])
        rel = sb("rel", [P, STEPS])
        wgt = sb("wgt", [P, STEPS])
        src_i = sb("src_i", [P, STEPS], I32)
        idx = sb("idx", [P, RING], I32)
        valid = sb("valid", [P, P])
        zeros_b = sb("zeros_b", [P, D], BF16)
        zeros = sb("zeros", [P, 512])
        ones_f = sb("ones_f", [P, 1])
        deg = sb("deg", [P, NT])
        dis = sb("dis", [P, NT])
        stats = sb("stats", [P, 6])
        mv = sb("mv", [P, NT, 2])
        rstd = sb("rstd", [P, NT])
        small = sb("small", [P, 4])
        bad = sb("bad", [P, D], I32)
        u = sb("u", [P, D])
        ut = sb("ut", [P, KD, P])
        y = sb("y", [P, D])
        z = sb("z", [P, D])
        wmat = sb("wmat", [P, 2, KD, D])
        vec = sb("vec", [P, 6, D])
        gwt = sb("gwt", [P, KD, EXPERTS])
        gbias = sb("gbias", [P, EXPERTS])
        scratch = sb("scratch", [P, 8])

        edges_in, x_in, small_in = sem("edges_in"), sem("x_in"), sem("small_in")
        consts, padded = sem("consts"), sem("padded")
        v = sem("vector_chain")
        var_ready, std_ready = sem("var_ready"), sem("std_ready")
        tiles_cmp, tiles_sum, first_ready, node_ps, pick_ready, step_ps = (
            sem(n) for n in ("tiles_cmp", "tiles_sum", "first_ready", "node_ps", "pick_ready", "step_ps"))

        with nc.Block() as block:
            @block.sync
            def _(sp):
                sp.wait_ge(padded, 4)
                for k, a in enumerate((dst, src)):
                    sp.dma_start(e_int[:, k, 0:EC - 1, :],
                                 a[0:(EC - 1) * P * P].rearrange("(c t p) -> t c p", t=P, p=P)).then_inc(edges_in, 16)
                    sp.dma_start(e_int[0:EFULL - (EC - 1) * P, k, EC - 1, :],
                                 a[(EC - 1) * P * P:EFULL * P].rearrange("(t p) -> t p", p=P)).then_inc(edges_in, 16)
                    sp.dma_start(e_int[EFULL - (EC - 1) * P:ET - (EC - 1) * P, k, EC - 1, 0:EREST],
                                 a[EFULL * P:E].rearrange("(t p) -> t p", t=1)).then_inc(edges_in, 16)
                a = edge_weight
                sp.dma_start(e_f[:, 2, 0:EC - 1, :],
                             a[0:(EC - 1) * P * P].rearrange("(c t p) -> t c p", t=P, p=P)).then_inc(edges_in, 16)
                sp.dma_start(e_f[0:EFULL - (EC - 1) * P, 2, EC - 1, :],
                             a[(EC - 1) * P * P:EFULL * P].rearrange("(t p) -> t p", p=P)).then_inc(edges_in, 16)
                sp.dma_start(e_f[EFULL - (EC - 1) * P:ET - (EC - 1) * P, 2, EC - 1, 0:EREST],
                             a[EFULL * P:E].rearrange("(t p) -> t p", t=1)).then_inc(edges_in, 16)
                sp.dma_start(xin[:, 0:NT - 1, :],
                             x[0:(NT - 1) * P, :].rearrange("(n p) d -> p n d", p=P)).then_inc(x_in, 16)
                sp.dma_start(xin[0:LAST, NT - 1, :], x[(NT - 1) * P:N, :]).then_inc(x_in, 16)
                for k, a in enumerate((g["gw1"], g["gw2"])):
                    sp.dma_start(wmat[:, k, :, :], a.rearrange("(k p) d -> p k d", p=P)).then_inc(small_in, 16)
                for k, name in enumerate(("gb1", "gg1", "gn1", "gb2", "gg2", "gn2")):
                    sp.dma_start(vec[:, k, :],
                                 g[name].rearrange("(a d) -> a d", a=1).to_broadcast([P, D])).then_inc(small_in, 16)
                sp.dma_start(gwt[:, :, :], g["gate_w"].rearrange("(k p) e -> p k e", p=P)).then_inc(small_in, 16)
                sp.dma_start(gbias[:, :],
                             g["gate_b"].rearrange("(a d) -> a d", a=1).to_broadcast([P, EXPERTS])).then_inc(small_in, 16)
                sp.wait_ge(consts, 11)
                for k in range(ROWS // P // 2):
                    sp.dma_start(rows_in[2 * P * k:2 * P * (k + 1), :].rearrange("(p a) d -> p (a d)", a=2),
                                 zeros[:, :]).then_inc(g["zeroed_rows"], 16)
                sp.wait_ge(small_in, 16 * 10)

            @block.gpsimd
            def _(pool):
                pool.memset(e_int[:, 0, EC - 1, :], 2 * NT * P).then_inc(padded, 1)
                pool.memset(e_int[:, 1, EC - 1, :], 0).then_inc(padded, 1)
                pool.memset(e_f[:, 2, EC - 1, :], 0.0).then_inc(padded, 1)
                pool.memset(xin[:, NT - 1, :], 0.0).then_inc(padded, 1)
                pool.memset(ident[:, :], 0.0).then_inc(consts, 1)
                pool.memset(ones[:, :], 1.0).then_inc(consts, 1)
                pool.memset(ones_f[:, :], 1.0).then_inc(consts, 1)
                pool.memset(eps[:, :], EPS).then_inc(consts, 1)
                pool.memset(below[:, :], 1.0).then_inc(consts, 1)
                pool.memset(valid[:, :], 1.0).then_inc(consts, 1)
                pool.memset(zeros[:, :], 0.0).then_inc(consts, 1)
                pool.memset(zeros_b[:, :], 0.0).then_inc(consts, 1)
                pool.iota(iota[:, :], pattern=[[1, STEPS]], base=0, channel_multiplier=0,
                          allow_small_or_imprecise_dtypes=True).then_inc(consts, 1)
                pool.iota(part[:, :], pattern=[[P, EC]], base=0, channel_multiplier=1,
                          allow_small_or_imprecise_dtypes=True).then_inc(consts, 1)
                pool.iota(bounds[:, :], pattern=[[P, NT]], base=0, channel_multiplier=0,
                          allow_small_or_imprecise_dtypes=True).then_inc(consts, 1)
                pool.wait_ge(consts, 11)
                pool.affine_select(out=ident[:, :], in_=ident[:, :], compare_op=ALU.not_equal, fill=1.0,
                                   base=0, pattern=[[-1, P]], channel_multiplier=1).then_inc(consts, 1)
                pool.affine_select(out=below[:, :], in_=below[:, :], compare_op=ALU.is_gt, fill=0.0,
                                   base=0, pattern=[[1, P]], channel_multiplier=-1).then_inc(consts, 1)
                pool.affine_select(out=valid[:, :], in_=valid[:, :], compare_op=ALU.is_gt, fill=0.0,
                                   base=E - (EC - 1) * P * P, pattern=[[-1, P]], channel_multiplier=-P).then_inc(consts, 1)

            @block.vector
            def _(dve):
                n = [0]

                def link(ins):
                    n[0] += 1
                    ins.then_inc(v, 1)
                    dve.wait_ge(v, n[0])

                dve.wait_ge(consts, 14)
                dve.wait_ge(edges_in, 16 * 9)
                link(dve.tensor_copy(e_f[:, 0:2, :, :], e_int[:, :, :, :]))
                for c in range(EC):
                    ins = dve.tensor_scalar(before[:, c, :], bounds[:, :], e_f[:, 0, c, P - 1:P], None, ALU.is_gt)
                ins.then_inc(tiles_cmp, 1)
                ew = e_f[:, 2, :, :]
                link(dve.tensor_scalar(bad_e[:, :, :], ew, 0.0, 0.0, ALU.mult, ALU.not_equal))
                link(dve.copy_predicated(ew, bad_e[:, :, :], zeros[:, :].rearrange("p (c q) -> p c q", c=EC)))
                link(dve.scalar_tensor_tensor(ew, ew, -1.0, ew, ALU.mult, ALU.max))
                link(dve.tensor_scalar(ew, ew, 1e-6, None, ALU.max))
                link(dve.tensor_tensor(e_f[:, 2, EC - 1, :], e_f[:, 2, EC - 1, :], valid[:, :], ALU.mult))
                dve.wait_ge(tiles_sum, 1)
                link(dve.tensor_scalar(first[0:NT, :], ps_b[0:NT, 0:1], part[0:NT, 0:1], None, ALU.add))
                dve.tensor_scalar(begun[0:NT, :], iota[0:NT, :], first[0:NT, 0:1], None, ALU.is_ge).then_inc(first_ready, 1)
                link(dve.memset(ends_f[:, NT - 1:NT], STEPS))
                link(dve.tensor_tensor(ends_f[:, 0:NT - 1], ps_a[:, 1:NT], iota[:, 1:NT], ALU.add))
                link(dve.tensor_scalar(ends_f[:, :], ends_f[:, :], float(RING), None, ALU.add))
                link(dve.tensor_copy(ends[:, 0:NT], ends_f[:, :]))
                dve.wait_ge(node_ps, 1)
                link(dve.tensor_scalar(node_of[:, :], ps_c[:, 0:STEPS], 1.0, None, ALU.subtract))
                link(dve.tensor_tensor(edge_of[:, :], iota[:, :], node_of[:, :], ALU.subtract))
                for c in range(EC):
                    ins = dve.tensor_scalar(pick[:, c, :], edge_of[:, :], part[:, c:c + 1], None, ALU.is_equal)
                ins.then_inc(pick_ready, 1)
                link(dve.tensor_copy(node_i[:, :], node_of[:, :]))
                link(dve.tensor_scalar(slot_off[:, :], node_i[:, :], SLOTS - 1, 9, ALU.bitwise_and, ALU.logical_shift_left))
                link(dve.tensor_scalar(node_next[:, :], node_of[:, :], 1.0, None, ALU.add))
                dve.wait_ge(step_ps, 1)
                link(dve.scalar_tensor_tensor(rel[:, :], node_of[:, :], -float(P), ps_d[:, 0:STEPS], ALU.mult, ALU.add))
                dve.tensor_copy(src_i[:, :], ps_b[:, 0:STEPS])
                link(dve.tensor_copy(wgt[:, :], ps_a[:, 0:STEPS]))
                dve.wait_ge(x_in, 32)
                for t in range(NT):
                    link(dve.bn_stats(stats[:, :], xin[:, t, :]))
                    ins = dve.bn_aggr(mv[:, t, :], stats[:, :])
                    if t < NT - 1:
                        link(ins)
                ins.then_inc(var_ready, 1)
                dve.wait_ge(std_ready, 1)
                link(dve.reciprocal(rstd[:, :], rstd[:, :]))
                for t in range(NT):
                    dve.tensor_scalar(h[:, t, :], xin[:, t, :], mv[:, t, 0:1], rstd[:, t:t + 1],
                                      ALU.subtract, ALU.mult).then_inc(v, 1)
                n[0] += NT
                dve.wait_ge(v, n[0])
                for t in range(NT):
                    link(dve.tensor_scalar(bad[:, :], h[:, t, :], 0.0, 0.0, ALU.mult, ALU.not_equal))
                    link(dve.copy_predicated(h[:, t, :], bad[:, :], zeros[:, 0:D]))

            @block.scalar
            def _(act):
                act.wait_ge(var_ready, 1)
                act.activation(rstd[:, :], mv[:, :, 1], ACT.Sqrt, bias=eps[:, 0:1]).then_inc(std_ready, 1)

            @block.tensor
            def _(pe):
                pe.wait_ge(tiles_cmp, 1)
                for c in range(EC):
                    pe.matmul(ps_a[:, 0:NT], ones[:, :], before[:, c, :], start=(c == 0), stop=(c == EC - 1))
                for c in range(EC):
                    mm = pe.matmul(ps_b[0:NT, 0:1], before[:, c, :], ones[:, 0:1], start=(c == 0), stop=(c == EC - 1))
                mm.then_inc(tiles_sum, 1)
                pe.wait_ge(first_ready, 1)
                pe.matmul(ps_c[:, 0:STEPS], ones[0:NT, :], begun[0:NT, :], start=True, stop=True).then_inc(node_ps, 1)
                pe.wait_ge(pick_ready, 1)
                for k, ps in ((0, ps_d), (1, ps_b), (2, ps_a)):
                    for c in range(EC):
                        mm = pe.matmul(ps[:, 0:STEPS], e_f[:, k, c, :], pick[:, c, :], start=(c == 0), stop=(c == EC - 1))
                mm.then_inc(step_ps, 1)

        ring_free = sem("ring_free")
        s_ready = sem("s_ready")
        landed = [sem(f"landed{k}") for k in range(RING)]
        slot_free = sem("slot_free")
        evac = sem("evac")
        staged = sem("staged")

        def edge_pass(q):
            base = STEPS * q
            width = D if q else 1
            with nc.Block() as block:
                @block.vector
                def _(dve):
                    if q == 0:
                        dve.memset(scratch[:, 0:1], 0.0).then_inc(ring_free, RING)
                    with dve.Fori(0, STEPS // RING) as i:
                        for k in range(RING):
                            if k % GROUP == 0:
                                dve.wait_ge(ring_free, i * RING + (base + k + GROUP))
                            dve.tensor_scalar(smat[:, k, :], iota[:, 0:P], rel[:, bass.ds(i * RING + k, 1)],
                                              wgt[:, bass.ds(i * RING + k, 1)], ALU.is_equal, ALU.mult).then_inc(s_ready, 1)

                if q:
                    @block.gpsimd
                    def _(pool):
                        with pool.Fori(0, STEPS // RING) as i:
                            for k in range(RING):
                                if k % GROUP == 0:
                                    pool.sem_clear(staged)
                                    pool.wait_ge(ring_free, i * RING + (base + k + GROUP))
                                    pool.tensor_tensor(scratch[:, 4:5], ones_f[:, :], ones_f[:, :], ALU.mult).then_inc(staged, 1)
                                    pool.tensor_copy(idx[:, k:k + GROUP],
                                                     src_i[:, bass.ds(i * RING + k, GROUP)]).then_inc(staged, 1)
                                    pool.wait_ge(staged, 2)
                                pool.indirect_dma_start(
                                    rows[:, k, :], None, table[:, :],
                                    bass.IndirectOffsetOnAxis(ap=idx[:, k:k + 1].bitcast(U32), axis=0)
                                ).then_inc(landed[k], 16)

                @block.tensor
                def _(pe):
                    for b in range(SLOTS):
                        mm = pe.matmul(ps_slot[:, SLOT * b:SLOT * b + width + width % 2], ones[:, :],
                                       zeros_b[:, 0:width + width % 2], start=True, stop=False, skip_group_check=True)
                    if q == 0:
                        mm.then_inc(slot_free, SLOTS)
                    regs = [pe.alloc_register(f"slot{q}_{k}") for k in range(GROUP)]
                    last = pe.alloc_register(f"last{q}")
                    with pe.Fori(0, STEPS // RING) as i:
                        for k in range(RING):
                            if k % GROUP == 0:
                                pe.reg_load(regs, slot_off[0:1, bass.ds(i * RING + k, GROUP)])
                                pe.reg_load(last, node_next[0:1, bass.ds(i * RING + (k + GROUP - 1), 1)])
                                pe.wait_ge(slot_free, pe.snap(last, min_val=1, max_val=NT) + NT * q)
                            pe.wait_ge(s_ready, i * RING + (base + k + 1))
                            if q:
                                pe.wait_ge(landed[k], i * 16 + 16 * (1 + (q - 1) * (STEPS // RING)))
                            off = pe.snap(regs[k % GROUP], min_val=0, max_val=(SLOTS - 1) * SLOT)
                            pe.matmul(ps_slot[:, bass.ds(off, width)], smat[:, k, :],
                                      rows[:, k, :] if q else ones_f[:, 0:1],
                                      start=False, stop=False, skip_group_check=True).then_inc(ring_free, 1)

                @block.scalar
                def _(act):
                    regs = [act.alloc_register(f"end{q}_{k}") for k in range(GROUP)]
                    for t in range(NT):
                        if t % GROUP == 0:
                            m = min(GROUP, NT - t)
                            act.reg_load(regs[0:m], ends[0:1, t:t + m])
                        s = (t % SLOTS) * SLOT
                        act.wait_ge(ring_free, act.snap(regs[t % GROUP], min_val=RING, max_val=RING + STEPS) + base)
                        target = sums[:, t, :] if q else deg[:, t:t + 1]
                        act.activation(target, ps_slot[:, s:s + width], ACT.Copy).then_inc(evac, 1)
                        act.wait_ge(evac, NT * q + t + 1)
                        act.activation(ps_slot[:, s:s + width], zeros[:, 0:width], ACT.Copy).then_inc(slot_free, 1)

        edge_pass(0)

        tv, table_out = sem("table_chain"), sem("table_out")
        with nc.Block() as block:
            @block.scalar
            def _(act):
                act.activation(dis[:, :], deg[:, :], ACT.Sqrt, bias=ones_f[:, 0:1]).then_inc(std_ready, 1)

            @block.vector
            def _(dve):
                dve.wait_ge(std_ready, 2)
                dve.reciprocal(dis[:, :], dis[:, :]).then_inc(tv, 1)
                dve.wait_ge(tv, 1)
                for t in range(NT):
                    dve.tensor_scalar(scaled[:, t, :], h[:, t, :], dis[:, t:t + 1], None, ALU.mult).then_inc(tv, 1)

            @block.sync
            def _(sp):
                for c in range(NT // UN):
                    sp.wait_ge(tv, 1 + UN * (c + 1))
                    sp.dma_start(table[UN * P * c:UN * P * (c + 1), :].rearrange("(n p) d -> p n d", p=P),
                                 scaled[:, UN * c:UN * (c + 1), :]).then_inc(table_out, 16)
                sp.wait_ge(table_out, 16 * (NT // UN))

        u_ready, turned, ut_ready, y_ps, y_taken = (
            sem(n) for n in ("u_ready", "turned", "ut_ready", "y_ps", "y_taken"))
        tile_done = sem("tile_done")
        x2_turned, x2t_ready, logit_ps, x2_ready = (
            sem(n) for n in ("x2_turned", "x2t_ready", "logit_ps", "x2_ready"))
        x2s = sb("x2s", [P, D])

        def post(q):
            layer = q - 1
            bias, gain, shift = vec[:, 3 * layer, :], vec[:, 3 * layer + 1, :], vec[:, 3 * layer + 2, :]
            base = NT * layer
            norms = layer + 1

            def nstd(i, k, j):
                return i * (UN * norms) + (3 + NT * layer + k * norms + j)
            with nc.Block() as block:
                @block.gpsimd
                def _(pool):
                    if layer == 0:
                        pool.memset(scratch[:, 3:4], 0.0).then_inc(turned, 1)
                    with pool.Fori(0, NT // UN) as i:
                        for k in range(UN):
                            pool.sem_clear(staged)
                            pool.wait_ge(turned, i * UN + (base + k + 1))
                            pool.tensor_tensor(scratch[:, 4:5], ones_f[:, :], ones_f[:, :], ALU.mult).then_inc(staged, 1)
                            pool.wait_ge(staged, 1)
                            pool.tensor_tensor(u[:, :], sums[:, bass.ds(i * UN + k, 1), :].rearrange("p a d -> p (a d)"),
                                               scaled[:, bass.ds(i * UN + k, 1), :].rearrange("p a d -> p (a d)"),
                                               ALU.add).then_inc(u_ready, 1)

                @block.tensor
                def _(pe):
                    with pe.Fori(0, NT // UN) as i:
                        for k in range(UN):
                            pe.wait_ge(u_ready, i * UN + (base + k + 1))
                            for c in range(KD):
                                mm = pe.transpose(ps_a[:, c * P:(c + 1) * P], u[:, c * P:(c + 1) * P], ident[:, :])
                            mm.then_inc(turned, 1)
                            pe.wait_ge(ut_ready, i * UN + (base + k + 1))
                            pe.wait_ge(y_taken, i * UN + (base + k + 1))
                            for c in range(KD):
                                mm = pe.matmul(ps_b[:, 0:D], ut[:, c, :], wmat[:, layer, c, :], start=(c == 0), stop=(c == KD - 1))
                            mm.then_inc(y_ps, 1)
                            if layer:
                                pe.wait_ge(x2_ready, i * UN + (k + 1))
                                for c in range(KD):
                                    mm = pe.transpose(ps_c[:, c * P:(c + 1) * P], x2s[:, c * P:(c + 1) * P], ident[:, :])
                                mm.then_inc(x2_turned, 1)
                                pe.wait_ge(x2t_ready, i * UN + (k + 1))
                                for c in range(KD):
                                    mm = pe.matmul(ps_d[:, 0:EXPERTS], x2t[:, c, :], gwt[:, c, :], start=(c == 0), stop=(c == KD - 1))
                                mm.then_inc(logit_ps, 1)

                @block.scalar
                def _(act):
                    with act.Fori(0, NT // UN) as i:
                        for k in range(UN):
                            act.wait_ge(turned, i * UN + (base + k + 2))
                            act.activation(ut[:, :, :].rearrange("p c q -> p (c q)"), ps_a[:, 0:D], ACT.Copy).then_inc(ut_ready, 1)
                            for j in range(norms):
                                act.wait_ge(var_ready, nstd(i, k, j) - 1)
                                act.activation(small[:, 2:3], small[:, 1:2], ACT.Sqrt, bias=eps[:, 0:1]).then_inc(std_ready, 1)
                            if layer:
                                act.wait_ge(x2_turned, i * UN + (k + 1))
                                act.activation(x2t[:, :, :].rearrange("p c q -> p (c q)"), ps_c[:, 0:D], ACT.Copy).then_inc(x2t_ready, 1)

                @block.vector
                def _(dve):
                    n = [0]

                    def link(ins):
                        n[0] += 1
                        ins.then_inc(v, 1)
                        dve.wait_ge(v, n[0])

                    def tile(a, t):
                        return a[:, bass.ds(t, 1), :].rearrange("p a d -> p (a d)")

                    if layer == 0:
                        dve.memset(scratch[:, 0:1], 0.0).then_inc(y_taken, 1)
                    with dve.Fori(0, NT // UN) as i:
                        dve.sem_clear(v)
                        n[0] = 0
                        for k in range(UN):
                            t = i * UN + k
                            dve.wait_ge(y_ps, i * UN + (base + k + 1))
                            ins = dve.scalar_tensor_tensor(y[:, :], ps_b[:, 0:D], dis[:, bass.ds(t, 1)], bias, ALU.mult, ALU.add)
                            ins.then_inc(y_taken, 1)
                            dve.wait_ge(y_taken, i * UN + (base + k + 2))
                            link(dve.tensor_scalar(bad[:, :], y[:, :], 0.0, 0.0, ALU.mult, ALU.not_equal))
                            link(dve.copy_predicated(y[:, :], bad[:, :], zeros[:, 0:D]))
                            link(dve.bn_stats(stats[:, :], y[:, :]))
                            dve.bn_aggr(small[:, 0:2], stats[:, :]).then_inc(var_ready, 1)
                            dve.wait_ge(std_ready, nstd(i, k, 0))
                            link(dve.reciprocal(small[:, 2:3], small[:, 2:3]))
                            link(dve.tensor_scalar(y[:, :], y[:, :], small[:, 0:1], small[:, 2:3], ALU.subtract, ALU.mult))
                            link(dve.tensor_tensor(y[:, :], y[:, :], gain, ALU.mult))
                            link(dve.tensor_tensor(y[:, :], y[:, :], shift, ALU.add))
                            link(dve.tensor_scalar(bad[:, :], y[:, :], 0.0, 0.0, ALU.mult, ALU.not_equal))
                            link(dve.copy_predicated(y[:, :], bad[:, :], zeros[:, 0:D]))
                            link(dve.scalar_tensor_tensor(z[:, :], y[:, :], 0.0, tile(h, t), ALU.max, ALU.add))
                            link(dve.tensor_scalar(bad[:, :], z[:, :], 0.0, 0.0, ALU.mult, ALU.not_equal))
                            link(dve.copy_predicated(z[:, :], bad[:, :], zeros[:, 0:D]))
                            if layer == 0:
                                dve.tensor_copy(tile(h, t), z[:, :])
                                dve.tensor_scalar(tile(scaled, t), z[:, :], dis[:, bass.ds(t, 1)], None,
                                                  ALU.mult).then_inc(tile_done, 1)
                            else:
                                link(dve.tensor_tensor(z[:, :], z[:, :], tile(xin, t), ALU.add))
                                dve.tensor_copy(tile(xin, t), z[:, :]).then_inc(tile_done, 1)
                                link(dve.bn_stats(stats[:, :], z[:, :]))
                                dve.bn_aggr(small[:, 0:2], stats[:, :]).then_inc(var_ready, 1)
                                dve.wait_ge(std_ready, nstd(i, k, 1))
                                link(dve.reciprocal(small[:, 2:3], small[:, 2:3]))
                                dve.tensor_scalar(x2s[:, :], z[:, :], small[:, 0:1], small[:, 2:3],
                                                  ALU.subtract, ALU.mult).then_inc(x2_ready, 1)
                                dve.wait_ge(x2_ready, i * UN + (k + 1))
                                link(dve.tensor_copy(tile(x2, t), x2s[:, :]))
                                dve.wait_ge(logit_ps, i * UN + (k + 1))
                                dve.tensor_tensor(tile(logits, t), ps_d[:, 0:EXPERTS], gbias[:, :], ALU.add)

                @block.sync
                def _(sp):
                    for c in range(NT // UN):
                        sp.wait_ge(tile_done, base + UN * (c + 1))
                        sp.dma_start((x1_dram if layer else table)[UN * P * c:UN * P * (c + 1), :].rearrange("(n p) d -> p n d", p=P),
                                     (xin if layer else scaled)[:, UN * c:UN * (c + 1), :]).then_inc(table_out, 16)
                    sp.wait_ge(table_out, 16 * (NT // UN) * (q + 1))

        x2t = sb("x2t", [P, KD, P])
        edge_pass(1)
        post(1)
        edge_pass(2)
        post(2)


def route(nc, sem, g, logits, sb):
    ones, below = g["ones"], g["below"]
    slot_id, top_w, w_off, ps_a, ps_b = g["slot_id"], g["top_w"], g["w_off"], g["ps_a"], g["ps_b"]
    one = [sb(f"one{k}", [P, NT, EXPERTS]) for k in range(2)]
    cand = sb("cand", [P, NT, EXPERTS])
    work = sb("work", [P, NT, EXPERTS])
    both = sb("both", [P, NT, EXPERTS], BF16)
    best = sb("best", [P, 2, NT])
    which = sb("which", [P, 2, NT])
    eids = sb("eids", [P, EXPERTS])
    live = sb("live", [P, NT])
    carry = sb("carry", [P, NT + 1, EXPERTS])
    count_i = sb("count_i", [P, EXPERTS], I32)
    nblk = sb("nblk", [P, 2, EXPERTS])
    blk_end = sb("blk_end", [P, EXPERTS])
    blk_start = sb("blk_start", [P, EXPERTS])
    bnum = sb("bnum", [P, BLOCKS])
    over = sb("over", [P, BLOCKS, EXPERTS])
    eid_b = sb("eid_b", [P, BLOCKS])
    slot_f = sb("slot_f", [P, 2, NT])
    gap = sb("gap", [P, NT])
    eg = sb("eg", [P, NT])
    neg = sb("neg", [P, NT, EXPERTS])
    flag = sb("flag", [P, NT, EXPERTS], I32)
    rc, ready, counted, v, ex = (sem(n) for n in ("route_consts", "route_onehot", "route_counted", "route_chain", "route_exp"))
    gapped = sem("route_gap")
    row = [P, NT, EXPERTS]

    def over_e(a):
        return a.rearrange("p (n e) -> p n e", e=1).to_broadcast(row)

    def over_n(a):
        return a.rearrange("p (n e) -> p n e", n=1).to_broadcast(row)

    with nc.Block() as block:
        @block.gpsimd
        def _(pool):
            pool.iota(eids[:, :], pattern=[[1, EXPERTS]], base=0, channel_multiplier=0,
                      allow_small_or_imprecise_dtypes=True).then_inc(rc, 1)
            pool.iota(bnum[:, :], pattern=[[1, BLOCKS]], base=0, channel_multiplier=0,
                      allow_small_or_imprecise_dtypes=True).then_inc(rc, 1)
            pool.memset(neg[:, :, :], -3.4e38).then_inc(rc, 1)
            pool.memset(live[:, :], 1.0).then_inc(rc, 1)
            pool.wait_ge(rc, 4)
            pool.affine_select(out=live[:, :], in_=live[:, :], compare_op=ALU.is_gt, fill=0.0, base=N,
                               pattern=[[-P, NT]], channel_multiplier=-1).then_inc(rc, 1)

        @block.tensor
        def _(pe):
            pe.wait_ge(ready, 1)
            both2 = both[:, :, :].rearrange("p n e -> p (n e)")
            pe.matmul(ps_a[:, 0:NT * EXPERTS], below[:, :], both2, start=True, stop=True)
            pe.matmul(ps_b[:, 0:NT * EXPERTS], ones[:, :], both2, start=True, stop=True).then_inc(counted, 1)

        @block.scalar
        def _(act):
            act.wait_ge(gapped, 1)
            act.activation(eg[:, :], gap[:, :], ACT.Exp).then_inc(ex, 1)

        @block.vector
        def _(dve):
            n = [0]

            def link(ins):
                n[0] += 1
                ins.then_inc(v, 1)
                dve.wait_ge(v, n[0])

            dve.wait_ge(rc, 5)
            for k in range(2):
                link(dve.tensor_reduce(best[:, k, :], logits[:, :, :], AX_X, ALU.max))
                link(dve.tensor_tensor(cand[:, :, :], logits[:, :, :], over_e(best[:, k, :]), ALU.is_equal))
                link(dve.tensor_scalar(cand[:, :, :], cand[:, :, :], -float(EXPERTS), float(EXPERTS), ALU.mult, ALU.add))
                link(dve.tensor_tensor(cand[:, :, :], cand[:, :, :], over_n(eids[:, :]), ALU.add))
                link(dve.tensor_reduce(which[:, k, :], cand[:, :, :], AX_X, ALU.min))
                link(dve.tensor_scalar(which[:, k, :], which[:, k, :], EXPERTS - 1.0, None, ALU.min))
                link(dve.tensor_tensor(one[k][:, :, :], over_n(eids[:, :]), over_e(which[:, k, :]), ALU.is_equal))
                if k == 0:
                    link(dve.tensor_copy(flag[:, :, :], one[0][:, :, :]))
                    link(dve.copy_predicated(logits[:, :, :], flag[:, :, :], neg[:, :, :]))
            dve.tensor_tensor(gap[:, :], best[:, 1, :], best[:, 0, :], ALU.subtract).then_inc(gapped, 1)
            link(dve.tensor_tensor(work[:, :, :], one[0][:, :, :], one[1][:, :, :], ALU.add))
            dve.tensor_tensor(both[:, :, :], work[:, :, :], over_e(live[:, :]), ALU.mult).then_inc(ready, 1)
            dve.wait_ge(ex, 1)
            link(dve.tensor_scalar(top_w[:, 0, :], eg[:, :], 1.0, None, ALU.add))
            link(dve.reciprocal(top_w[:, 0, :], top_w[:, 0, :]))
            link(dve.tensor_tensor(top_w[:, 1, :], top_w[:, 0, :], eg[:, :], ALU.mult))
            link(dve.memset(carry[:, 0, :], 0.0))
            dve.wait_ge(counted, 1)
            for t in range(NT):
                link(dve.tensor_tensor(carry[:, t + 1, :], carry[:, t, :], ps_b[:, t * EXPERTS:(t + 1) * EXPERTS], ALU.add))
            link(dve.tensor_scalar(nblk[:, 0, :], carry[:, NT, :], P - 1.0, None, ALU.add))
            link(dve.tensor_copy(count_i[:, :], nblk[:, 0, :]))
            link(dve.tensor_scalar(count_i[:, :], count_i[:, :], 7, None, ALU.logical_shift_right))
            link(dve.tensor_copy(nblk[:, 1, :], count_i[:, :]))
            link(dve.tensor_copy(blk_end[:, :], nblk[:, 1, :]))
            for e in range(1, EXPERTS):
                link(dve.tensor_tensor(blk_end[:, e:e + 1], blk_end[:, e:e + 1], blk_end[:, e - 1:e], ALU.add))
            link(dve.tensor_tensor(blk_start[:, :], blk_end[:, :], nblk[:, 1, :], ALU.subtract))
            link(dve.tensor_scalar(blk_start[:, :], blk_start[:, :], float(P), None, ALU.mult))
            link(dve.tensor_tensor(work[:, :, :], carry[:, 0:NT, :],
                                   ps_a[:, 0:NT * EXPERTS].rearrange("p (n e) -> p n e", e=EXPERTS), ALU.add))
            link(dve.tensor_tensor(work[:, :, :], work[:, :, :], over_n(blk_start[:, :]), ALU.add))
            for k in range(2):
                link(dve.tensor_tensor(cand[:, :, :], work[:, :, :], one[k][:, :, :], ALU.mult))
                link(dve.tensor_reduce(slot_f[:, k, :], cand[:, :, :], AX_X, ALU.add))
            link(dve.tensor_copy(slot_id[:, :, :], slot_f[:, :, :]))
            wide = [P, BLOCKS, EXPERTS]
            link(dve.tensor_tensor(over[:, :, :], bnum[:, :].rearrange("p (b e) -> p b e", e=1).to_broadcast(wide),
                                   blk_end[:, :].rearrange("p (b e) -> p b e", b=1).to_broadcast(wide), ALU.is_ge))
            link(dve.tensor_reduce(eid_b[:, :], over[:, :, :], AX_X, ALU.add))
            link(dve.tensor_scalar(eid_b[:, :], eid_b[:, :], EXPERTS - 1.0, None, ALU.min))
            link(dve.tensor_copy(w_off[:, :], eid_b[:, :]))


def experts(nc, sem, g):
    ident, x2, slot_id, top_w, w_off = g["ident"], g["x2"], g["slot_id"], g["top_w"], g["w_off"]
    rows_in, rows_out, x1_dram, out = g["rows_in"], g["rows_out"], g["x1_dram"], g["out"]
    ps_slot, ps_a, ps_b, ps_c, ps_d = g["ps_slot"], g["ps_a"], g["ps_b"], g["ps_c"], g["ps_d"]
    ring = 4
    with ExitStack() as ctx:
        def sb(name, shape, dt=F32):
            return ctx.enter_context(nc.sbuf_tensor(name, shape, dt))

        with ExitStack() as inner:
            def sbi(name, shape, dt=F32):
                return inner.enter_context(nc.sbuf_tensor(name, shape, dt))
            w1 = sbi("w1", [P, EXPERTS * KD * F])
            w2 = sbi("w2", [P, EXPERTS * KF * D])
            b1r = sbi("b1r", [EXPERTS * KF, P])
            b1t = sbi("b1t", [P, EXPERTS * KF])
            b2b = sbi("b2b", [P, EXPERTS * D])
            xb = sbi("xb", [P, ring, D])
            xt = sbi("xt", [P, 2, KD, P])
            hid = sbi("hid", [P, 2, F])
            hidt = sbi("hidt", [P, 2, KF, P])
            yb = sbi("yb", [P, 2, D])

            scattered, w_in, b_in = sem("scattered"), sem("w_in"), sem("b_in")
            b1_ps, b1_ready = sem("b1_ps"), sem("b1_ready")
            xb_in = [sem(f"xb_in{k}") for k in range(ring)]
            x_turned, xt_ready, h_ps, hid_ready, h_turned, hidt_ready, out_ps, y_ready = (
                sem(n) for n in ("x_turned", "xt_ready", "h_ps", "hid_ready", "h_turned", "hidt_ready", "out_ps", "y_ready"))
            y_out = [sem(f"y_out{k}") for k in range(2)]
            B4 = 4
            with nc.Block() as block:
                @block.gpsimd
                def _(pool):
                    pool.wait_ge(g["zeroed_rows"], 16 * (ROWS // P // 2))
                    for t in range(NT):
                        m = P if t < NT - 1 else LAST
                        for k in range(2):
                            pool.indirect_dma_start(
                                rows_in[:, :], bass.IndirectOffsetOnAxis(ap=slot_id[0:m, k, t:t + 1].bitcast(U32), axis=0),
                                x2[0:m, t, :], None).then_inc(scattered, 16)
                    pool.wait_ge(scattered, 32 * NT)

                @block.sync
                def _(sp):
                    for e in range(EXPERTS):
                        sp.dma_start(w1[:, e * KD * F:(e + 1) * KD * F].rearrange("p (k f) -> p k f", k=KD),
                                     g["ew1"][e].rearrange("(k p) f -> p k f", p=P)).then_inc(w_in, 16)
                    sp.dma_start(b1r[:, :], g["eb1"].rearrange("e (c p) -> (e c) p", p=P)).then_inc(b_in, 16)
                    sp.dma_start(b2b[:, :], g["eb2"].rearrange("(a e) d -> a (e d)", a=1).to_broadcast([P, EXPERTS * D])).then_inc(b_in, 16)
                    for e in range(EXPERTS):
                        sp.dma_start(w2[:, e * KF * D:(e + 1) * KF * D].rearrange("p (k f) -> p k f", k=KF),
                                     g["ew2"][e].rearrange("(k p) f -> p k f", p=P)).then_inc(w_in, 16)
                    sp.wait_ge(scattered, 32 * NT)

                    def load(b, k):
                        sp.dma_start(xb[:, k, :], rows_in[bass.ds(b * P, P), :]).then_inc(xb_in[k], 16)

                    def store(b, k):
                        sp.wait_ge(y_ready, b + 3)
                        sp.dma_start(rows_out[bass.ds(b * P, P), :], yb[:, k % 2, :]).then_inc(y_out[k % 2], 16)

                    for k in range(ring):
                        load(k, k)
                    with sp.Fori(0, BLOCKS // ring - 1) as i:
                        for k in range(ring):
                            sp.wait_ge(x_turned, i * ring + (k + 1))
                            load(i * ring + (k + ring), k)
                            store(i * ring + k, k)
                    for k in range(ring):
                        store(BLOCKS - ring + k, k)
                    for k in range(2):
                        sp.wait_ge(y_out[k], 16 * (BLOCKS // 2 + 1))

                px, ph, pt, py = ([ps_slot[:, (2 * j + k) * BANK:(2 * j + k) * BANK + w] for k in range(2)]
                                  for j, w in enumerate((D, F, F, D)))
                pb = ps_slot[:, 0:EXPERTS * KF]

                @block.tensor
                def _(pe):
                    pe.wait_ge(b_in, 32)
                    pe.transpose(pb, b1r[:, :], ident[0:EXPERTS * KF, 0:EXPERTS * KF]).then_inc(b1_ps, 1)
                    pe.wait_ge(b1_ready, 1)
                    regs = [pe.alloc_register(f"expert{k}") for k in range(ring + 2)]

                    def turn_x(b, q, loads):
                        pe.wait_ge(xb_in[q], loads * 16)
                        for c in range(KD):
                            mm = pe.transpose(px[q % 2][:, c * P:(c + 1) * P], xb[:, q, c * P:(c + 1) * P], ident[:, :])
                        mm.then_inc(x_turned, 1)

                    def up(b, q, e):
                        pe.wait_ge(xt_ready, b + 1)
                        for c in range(KD):
                            mm = pe.matmul(ph[q % 2], xt[:, q % 2, c, :], w1[:, bass.ds(e * (KD * F) + c * F, F)],
                                           start=(c == 0), stop=(c == KD - 1))
                        mm.then_inc(h_ps, 1)

                    def turn_h(b, q):
                        pe.wait_ge(hid_ready, b + 1)
                        for c in range(KF):
                            mm = pe.transpose(pt[q % 2][:, c * P:(c + 1) * P], hid[:, q % 2, c * P:(c + 1) * P], ident[:, :])
                        mm.then_inc(h_turned, 1)

                    def down(b, q, e):
                        pe.wait_ge(hidt_ready, b + 1)
                        pe.wait_ge(y_ready, b + 1)
                        for c in range(KF):
                            mm = pe.matmul(py[q % 2], hidt[:, q % 2, c, :], w2[:, bass.ds(e * (KF * D) + c * D, D)],
                                           start=(c == 0), stop=(c == KF - 1))
                        mm.then_inc(out_ps, 1)

                    def expert(k):
                        return pe.snap(regs[k], min_val=0, max_val=EXPERTS - 1)

                    turn_x(0, 0, 1)
                    turn_x(1, 1, 1)
                    pe.wait_ge(w_in, 32 * EXPERTS)
                    pe.reg_load(regs[0:3], w_off[0:1, 0:3])
                    first = [expert(k) for k in range(3)]
                    up(0, 0, first[0])
                    up(1, 1, first[1])
                    turn_h(0, 0)
                    turn_x(2, 2, 1)
                    up(2, 2, first[2])
                    turn_h(1, 1)
                    down(0, 0, first[0])
                    turn_x(3, 3, 1)
                    with pe.Fori(0, BLOCKS // ring - 1) as i:
                        pe.reg_load(regs, w_off[0:1, bass.ds(i * ring + 1, ring + 2)])
                        for k in range(ring):
                            b = i * ring + (2 + k)
                            up(b + 1, (3 + k) % ring, expert(k + 2))
                            turn_h(b, (2 + k) % ring)
                            down(b - 1, (1 + k) % ring, expert(k))
                            turn_x(b + 2, k, i + 2)
                    pe.reg_load(regs[0:3], w_off[0:1, BLOCKS - 3:BLOCKS])
                    last = [expert(k) for k in range(3)]
                    b = BLOCKS - 2
                    up(b + 1, (b + 1) % ring, last[2])
                    turn_h(b, b % ring)
                    down(b - 1, (b - 1) % ring, last[0])
                    turn_h(b + 1, (b + 1) % ring)
                    down(b, b % ring, last[1])
                    down(b + 1, (b + 1) % ring, last[2])

                @block.scalar
                def _(act):
                    act.wait_ge(b1_ps, 1)
                    act.activation(b1t[:, :], pb, ACT.Copy).then_inc(b1_ready, 1)

                    def copy_x(b, s):
                        act.wait_ge(x_turned, b + 1)
                        act.activation(xt[:, s, :, :].rearrange("p c q -> p (c q)"), px[s], ACT.Copy).then_inc(xt_ready, 1)

                    def copy_h(b, s):
                        act.wait_ge(h_ps, b + 1)
                        act.activation(hid[:, s, :], ph[s], ACT.Copy).then_inc(hid_ready, 1)

                    copy_x(0, 0)
                    copy_x(1, 1)
                    copy_h(0, 0)
                    with act.Fori(0, BLOCKS // 2 - 1) as i:
                        for k in range(2):
                            copy_h(i * 2 + (1 + k), (1 + k) % 2)
                            copy_x(i * 2 + (2 + k), k)
                    copy_h(BLOCKS - 1, 1)

                @block.vector
                def _(dve):
                    dve.memset(yb[:, 0, 0:1], 0.0).then_inc(y_ready, 2)
                    dve.memset(yb[:, 0, 1:2], 0.0).then_inc(y_out[0], 16)
                    dve.memset(yb[:, 0, 2:3], 0.0).then_inc(y_out[1], 16)
                    dve.wait_ge(y_out[1], 16)
                    dve.wait_ge(b_in, 32)
                    dve.wait_ge(b1_ready, 1)
                    regs = [dve.alloc_register(f"expert_v{k}") for k in range(3)]

                    def relu_h(b, s, e):
                        dve.wait_ge(h_turned, b + 1)
                        for c in range(KF):
                            ins = dve.tensor_scalar(hidt[:, s, c, :], pt[s][:, c * P:(c + 1) * P],
                                                    b1t[:, bass.ds(e * KF + c, 1)], 0.0, ALU.add, ALU.max)
                        ins.then_inc(hidt_ready, 1)

                    def add_b2(b, s, e, uses):
                        dve.wait_ge(y_out[s], uses * 16)
                        dve.wait_ge(out_ps, b + 1)
                        dve.tensor_tensor(yb[:, s, :], py[s], b2b[:, bass.ds(e * D, D)], ALU.add).then_inc(y_ready, 1)

                    def expert(k):
                        return dve.snap(regs[k], min_val=0, max_val=EXPERTS - 1)

                    dve.reg_load(regs[0:2], w_off[0:1, 0:2])
                    relu_h(0, 0, expert(0))
                    relu_h(1, 1, expert(1))
                    add_b2(0, 0, expert(0), 1)
                    with dve.Fori(0, BLOCKS // 2 - 1) as i:
                        dve.reg_load(regs, w_off[0:1, bass.ds(i * 2 + 1, 3)])
                        for k in range(2):
                            relu_h(i * 2 + (2 + k), k, expert(k + 1))
                            add_b2(i * 2 + (1 + k), (1 + k) % 2, expert(k), i + (1 + k))
                    dve.reg_load(regs[0:1], w_off[0:1, BLOCKS - 1:BLOCKS])
                    add_b2(BLOCKS - 1, 1, expert(0), BLOCKS // 2)

        combine(nc, sem, g, sb)


def combine(nc, sem, g, sb):
    x2, slot_id, top_w, rows_out, x1_dram, out = (g[n] for n in ("x2", "slot_id", "top_w", "rows_out", "x1_dram", "out"))
    ya = sb("ya", [P, UN, 2, D])
    x1t = sb("x1t", [P, UN, D])
    y_sum = sb("y_sum", [P, UN, D])
    res = sb("res", [P, UN, D])
    gam = sb("gam", [P, D])
    bet = sb("bet", [P, D])
    stats = sb("stats2", [P, 6])
    small = sb("small2", [P, 4])
    fetched = [sem(f"fetched{k}") for k in range(UN)]
    x1_in = [sem(f"x1_in{k}") for k in range(UN)]
    stored = [sem(f"stored{k}") for k in range(UN)]
    var_ready, std_ready = sem("var_ready2"), sem("std_ready2")
    padded, gb_in, cv, done = sem("padded2"), sem("gb_in"), sem("combine_chain"), sem("combined")
    with nc.Block() as block:
        @block.gpsimd
        def _(pool):
            pool.memset(ya[:, UN - 1, :, :], 0.0).then_inc(padded, 1)
            pool.wait_ge(padded, 1)
            for t in range(NT):
                m = P if t < NT - 1 else LAST
                if t >= UN:
                    pool.wait_ge(done, t - UN + 1)
                for k in range(2):
                    pool.indirect_dma_start(
                        ya[0:m, t % UN, k, :], None, rows_out[:, :],
                        bass.IndirectOffsetOnAxis(ap=slot_id[0:m, k, t:t + 1].bitcast(U32), axis=0)
                    ).then_inc(fetched[t % UN], 16)

        @block.sync
        def _(sp):
            sp.dma_start(gam[:, :], g["gamma"].rearrange("(a d) -> a d", a=1).to_broadcast([P, D])).then_inc(gb_in, 16)
            sp.dma_start(bet[:, :], g["beta"].rearrange("(a d) -> a d", a=1).to_broadcast([P, D])).then_inc(gb_in, 16)
            for t in range(NT + UN - 1):
                if t < NT:
                    if t >= UN:
                        sp.wait_ge(done, t - UN + 1)
                    sp.dma_start(x1t[:, t % UN, :], x1_dram[t * P:(t + 1) * P, :]).then_inc(x1_in[t % UN], 16)
                d = t - (UN - 1)
                if d >= 0:
                    m = P if d < NT - 1 else LAST
                    sp.wait_ge(done, d + 1)
                    sp.dma_start(out[d * P:d * P + m, :], res[0:m, d % UN, :]).then_inc(stored[d % UN], 16)
            for k in range(UN):
                sp.wait_ge(stored[k], 16 * (NT // UN + 1))

        @block.scalar
        def _(act):
            with act.Fori(0, NT // UN) as i:
                for k in range(UN):
                    act.wait_ge(var_ready, i * UN + (k + 1))
                    act.activation(small[:, 2:3], small[:, 1:2], ACT.Sqrt, bias=g["eps"][:, 0:1]).then_inc(std_ready, 1)

        @block.vector
        def _(dve):
            for k in range(UN):
                dve.memset(res[:, k, 0:1], 0.0).then_inc(stored[k], 16)
            dve.wait_ge(stored[UN - 1], 16)
            dve.wait_ge(gb_in, 32)
            with dve.Fori(0, NT // UN) as i:
                dve.sem_clear(cv)
                n = [0]

                def link(ins):
                    n[0] += 1
                    ins.then_inc(cv, 1)
                    dve.wait_ge(cv, n[0])

                for k in range(UN):
                    t = i * UN + k
                    y = y_sum[:, k, :]
                    x2t = x2[:, bass.ds(t, 1), :].rearrange("p a d -> p (a d)")
                    dve.wait_ge(fetched[k], i * 32 + 32)
                    link(dve.scalar_tensor_tensor(y, ya[:, k, 0, :], top_w[:, 0, bass.ds(t, 1)], x2t, ALU.mult, ALU.add))
                    link(dve.scalar_tensor_tensor(y, ya[:, k, 1, :], top_w[:, 1, bass.ds(t, 1)], y, ALU.mult, ALU.add))
                    link(dve.bn_stats(stats[:, :], y))
                    dve.bn_aggr(small[:, 0:2], stats[:, :]).then_inc(var_ready, 1)
                    dve.wait_ge(std_ready, i * UN + (k + 1))
                    link(dve.reciprocal(small[:, 2:3], small[:, 2:3]))
                    link(dve.tensor_scalar(y, y, small[:, 0:1], small[:, 2:3], ALU.subtract, ALU.mult))
                    link(dve.tensor_tensor(y, y, gam[:, :], ALU.mult))
                    link(dve.tensor_tensor(y, y, bet[:, :], ALU.add))
                    dve.wait_ge(x1_in[k], i * 16 + 16)
                    dve.wait_ge(stored[k], i * 16 + 16)
                    dve.tensor_tensor(res[:, k, :], y, x1t[:, k, :], ALU.add).then_inc(done, 1)


_INS = ["x", "src", "dst", "edge_weight", "L0_gnn_W1", "L0_gnn_b1", "L0_gnn_ln_g1", "L0_gnn_ln_b1", "L0_gnn_W2",
        "L0_gnn_b2", "L0_gnn_ln_g2", "L0_gnn_ln_b2", "L0_ffn_gate_w", "L0_ffn_gate_b", "L0_ffn_w1", "L0_ffn_b1",
        "L0_ffn_w2", "L0_ffn_b2", "L0_ffn_gamma", "L0_ffn_beta"]


def kernel(**inputs):
    import numpy as _np
    import concourse.bacc as _bacc
    from concourse import mybir as _mybir
    from concourse.bass_utils import run_bass_kernel_spmd as _run

    nc = _bacc.Bacc("TRN2", target_bir_lowering=False, num_devices=1)
    arrays, args = {}, []
    for name in _INS:
        a = _np.ascontiguousarray(inputs[name])
        arrays[f"in_{name}_dram"] = a
        args.append(nc.dram_tensor(f"in_{name}_dram", a.shape, _mybir.dt.from_np(a.dtype), kind="ExternalInput").ap())
    args.append(nc.dram_tensor("out_0_dram", (N, D), _mybir.dt.float32, kind="ExternalOutput").ap())
    program(nc, *args)
    r = _run(nc, [arrays], core_ids=[0])
    return r.results[0]["out_0_dram"]
```

```python
from contextlib import ExitStack

import concourse.bass as bass
from concourse import mybir

F32 = mybir.dt.float32
BF16 = mybir.dt.bfloat16
I32 = mybir.dt.int32
U32 = mybir.dt.uint32
U16 = mybir.dt.uint16
ALU = mybir.AluOpType
ACT = mybir.ActivationFunctionType
AX_X = mybir.AxisListType.X

P = 128
N, D, E = 3125, 256, 50000
EXPERTS, F = 16, 512
EPS = 1e-5
KD, KF = D // P, F // P
NT = -(-N // P)
LAST = N - (NT - 1) * P
ET = -(-E // P)
EFULL = E // P
EREST = E - EFULL * P
EC = -(-ET // P)
GROUP = 8
RING = 2 * GROUP
STEPS = -(-(ET + NT - 1) // RING) * RING
BANKS, BANK = 8, 512
SLOTS, SLOT = 4, BANK
ITERS = STEPS // RING
FLUSH = 3
UNITS = ITERS + NT
UN = 5
BLOCKS = (2 * N + EXPERTS * (P - 1)) // P
ROWS = BLOCKS * P


def program(nc, x, src, dst, edge_weight, gw1, gb1, gg1, gn1, gw2, gb2, gg2, gn2,
            gate_w, gate_b, ew1, eb1, ew2, eb2, gamma, beta, out):
    tables = [nc.dram_tensor(f"scaled_rows{k}", ((NT + 1) * P, D), F32, kind="Internal").ap() for k in range(2)]
    x1_dram = nc.dram_tensor("after_gnn", ((NT + 1) * P, D), F32, kind="Internal").ap()
    rows_in = nc.dram_tensor("expert_rows_in", (ROWS, D), F32, kind="Internal").ap()
    rows_out = nc.dram_tensor("expert_rows_out", (ROWS, D), F32, kind="Internal").ap()

    with ExitStack() as outer:
        def sem(name):
            return outer.enter_context(nc.semaphore(name))

        def keep(name, shape, dt=F32):
            return outer.enter_context(nc.sbuf_tensor(name, shape, dt))

        ident = keep("ident", [P, P])
        eps = keep("eps", [P, 1])
        ones = keep("ones", [P, P], BF16)
        below = keep("below", [P, P], BF16)
        x2 = keep("x2", [P, NT + 1, D])
        slot_id = keep("slot_id", [P, 2, NT], I32)
        top_w = keep("top_w", [P, 2, NT])
        logits = keep("logits", [P, NT, EXPERTS])
        w_off = keep("w_off", [P, BLOCKS], I32)
        ps = outer.enter_context(nc.psum_tensor("ps", [P, BANKS * BANK], F32))
        ps_slot = ps[:, :]
        ps_a, ps_b, ps_c, ps_d = (ps[:, k * BANK:(k + 1) * BANK] for k in range(4))

        zeroed_rows = sem("zeroed_rows")

        gnn(nc, sem, locals())
        with ExitStack() as ctx:
            route(nc, sem, locals(), logits,
                  lambda name, shape, dt=F32: ctx.enter_context(nc.sbuf_tensor(name, shape, dt)))
        experts(nc, sem, locals())


def gnn(nc, sem, g):
    x, src, dst, edge_weight = g["x"], g["src"], g["dst"], g["edge_weight"]
    ident, ones, below, x2 = g["ident"], g["ones"], g["below"], g["x2"]
    tables, x1_dram, rows_in = g["tables"], g["x1_dram"], g["rows_in"]
    ps_slot, ps_a, ps_b, ps_c, ps_d = g["ps_slot"], g["ps_a"], g["ps_b"], g["ps_c"], g["ps_d"]
    logits, eps = g["logits"], g["eps"]
    with ExitStack() as ctx:
        def sb(name, shape, dt=F32):
            return ctx.enter_context(nc.sbuf_tensor(name, shape, dt))

        h = sb("h", [P, NT + 1, D])
        xin = sb("xin", [P, NT + 1, D])
        scaled = sb("scaled", [P, NT + 1, D])
        sums = sb("sums", [P, NT + 1, D])
        iota = sb("iota", [P, STEPS])
        node_next = sb("node_next", [P, STEPS], U16)
        slot_off = sb("slot_off", [P, STEPS], I32)
        ends = sb("ends", [P, 32], U16)
        rel = sb("rel", [P, STEPS])
        wgt = sb("wgt", [P, STEPS])
        src_i = sb("src_i", [P, STEPS], I32)
        zeros_b = sb("zeros_b", [P, D], BF16)
        zeros = sb("zeros", [P, 512])
        ones_f = sb("ones_f", [P, 1])
        deg = sb("deg", [P, NT])
        dis = sb("dis", [P, NT + 1])
        stats = sb("stats", [P, 6])
        mv = sb("mv", [P, NT, 2])
        rstd = sb("rstd", [P, NT])
        small = sb("small", [P, 8])
        wmat = sb("wmat", [P, 2, KD, D])
        vec = sb("vec", [P, 6, D])
        gwt = sb("gwt", [P, KD, EXPERTS])
        gbias = sb("gbias", [P, EXPERTS])
        scratch = sb("scratch", [P, 8])

        unit_tile = sb("unit_tile", [P, UNITS + 1], I32)
        unit_wait = sb("unit_wait", [P, UNITS + 1], U16)
        left = sb("left", [P, 1], I32)

        setup_mem = ctx.enter_context(ExitStack())

        def tmp(name, shape, dt=F32):
            return setup_mem.enter_context(nc.sbuf_tensor(name, shape, dt))

        e_int = tmp("e_int", [P, 2, EC, P], I32)
        e_f = tmp("e_f", [P, 3, EC, P])
        bad_e = tmp("bad_e", [P, EC, P], I32)
        part = tmp("part", [P, EC])
        bounds = tmp("bounds", [P, NT])
        before = tmp("before", [P, EC, NT], BF16)
        first = tmp("first", [P, 1])
        begun = tmp("begun", [P, STEPS], BF16)
        node_of = tmp("node_of", [P, STEPS])
        edge_of = tmp("edge_of", [P, STEPS])
        pick = tmp("pick", [P, EC, STEPS])
        node_i = tmp("node_i", [P, STEPS], I32)
        ends_f = tmp("ends_f", [P, NT])
        valid = tmp("valid", [P, P])
        hot = tmp("hot", [P, RING, P], BF16)
        iota_b = tmp("iota_b", [P, P], BF16)
        w_parts = tmp("w_parts", [P, STEPS, 4], BF16)
        w_rest = tmp("w_rest", [P, STEPS])
        deg_off = tmp("deg_off", [P, STEPS], I32)
        node_of4 = tmp("node_of4", [P, STEPS])
        w_group = tmp("w_group", [P, RING // GROUP, GROUP, 4], BF16)
        rel_group = tmp("rel_group", [P, RING // GROUP, GROUP])
        begun_units = tmp("begun_units", [P, UNITS + 1])
        complete = tmp("complete", [P, UNITS])
        plus_one = tmp("plus_one", [P, UNITS])
        unit_f = tmp("unit_f", [P, UNITS])
        taken = tmp("taken", [P, UNITS])
        shift0 = tmp("shift0", [P, NT])

        edges_in, x_in, small_in = sem("edges_in"), sem("x_in"), sem("small_in")
        consts, padded, spare = sem("consts"), sem("padded"), sem("spare")
        v = sem("vector_chain")
        var_ready, std_ready = sem("var_ready"), sem("std_ready")
        tiles_cmp, tiles_sum, first_ready, node_ps, pick_ready, step_ps = (
            sem(n) for n in ("tiles_cmp", "tiles_sum", "first_ready", "node_ps", "pick_ready", "step_ps"))

        with nc.Block() as block:
            @block.sync
            def _(sp):
                sp.wait_ge(padded, 4)
                for k, a in enumerate((dst, src)):
                    sp.dma_start(e_int[:, k, 0:EC - 1, :],
                                 a[0:(EC - 1) * P * P].rearrange("(c t p) -> t c p", t=P, p=P)).then_inc(edges_in, 16)
                    sp.dma_start(e_int[0:EFULL - (EC - 1) * P, k, EC - 1, :],
                                 a[(EC - 1) * P * P:EFULL * P].rearrange("(t p) -> t p", p=P)).then_inc(edges_in, 16)
                    sp.dma_start(e_int[EFULL - (EC - 1) * P:ET - (EC - 1) * P, k, EC - 1, 0:EREST],
                                 a[EFULL * P:E].rearrange("(t p) -> t p", t=1)).then_inc(edges_in, 16)
                a = edge_weight
                sp.dma_start(e_f[:, 2, 0:EC - 1, :],
                             a[0:(EC - 1) * P * P].rearrange("(c t p) -> t c p", t=P, p=P)).then_inc(edges_in, 16)
                sp.dma_start(e_f[0:EFULL - (EC - 1) * P, 2, EC - 1, :],
                             a[(EC - 1) * P * P:EFULL * P].rearrange("(t p) -> t p", p=P)).then_inc(edges_in, 16)
                sp.dma_start(e_f[EFULL - (EC - 1) * P:ET - (EC - 1) * P, 2, EC - 1, 0:EREST],
                             a[EFULL * P:E].rearrange("(t p) -> t p", t=1)).then_inc(edges_in, 16)
                sp.dma_start(xin[:, 0:NT - 1, :],
                             x[0:(NT - 1) * P, :].rearrange("(n p) d -> p n d", p=P)).then_inc(x_in, 16)
                sp.dma_start(xin[0:LAST, NT - 1, :], x[(NT - 1) * P:N, :]).then_inc(x_in, 16)
                for k, a in enumerate((g["gw1"], g["gw2"])):
                    sp.dma_start(wmat[:, k, :, :], a.rearrange("(k p) d -> p k d", p=P)).then_inc(small_in, 16)
                for k, name in enumerate(("gb1", "gg1", "gn1", "gb2", "gg2", "gn2")):
                    sp.dma_start(vec[:, k, :],
                                 g[name].rearrange("(a d) -> a d", a=1).to_broadcast([P, D])).then_inc(small_in, 16)
                sp.dma_start(gwt[:, :, :], g["gate_w"].rearrange("(k p) e -> p k e", p=P)).then_inc(small_in, 16)
                sp.dma_start(gbias[:, :],
                             g["gate_b"].rearrange("(a d) -> a d", a=1).to_broadcast([P, EXPERTS])).then_inc(small_in, 16)
                sp.wait_ge(consts, 11)
                for k in range(ROWS // P // 2):
                    sp.dma_start(rows_in[2 * P * k:2 * P * (k + 1), :].rearrange("(p a) d -> p (a d)", a=2),
                                 zeros[:, :]).then_inc(g["zeroed_rows"], 16)
                sp.wait_ge(small_in, 16 * 10)

            @block.gpsimd
            def _(pool):
                pool.memset(e_int[:, 0, EC - 1, :], 2 * NT * P).then_inc(padded, 1)
                pool.memset(e_int[:, 1, EC - 1, :], 0).then_inc(padded, 1)
                pool.memset(e_f[:, 2, EC - 1, :], 0.0).then_inc(padded, 1)
                pool.memset(xin[:, NT - 1, :], 0.0).then_inc(padded, 1)
                pool.memset(ident[:, :], 0.0).then_inc(consts, 1)
                pool.memset(ones[:, :], 1.0).then_inc(consts, 1)
                pool.memset(ones_f[:, :], 1.0).then_inc(consts, 1)
                pool.memset(eps[:, :], EPS).then_inc(consts, 1)
                pool.memset(below[:, :], 1.0).then_inc(consts, 1)
                pool.memset(valid[:, :], 1.0).then_inc(consts, 1)
                pool.memset(zeros[:, :], 0.0).then_inc(consts, 1)
                pool.memset(zeros_b[:, :], 0.0).then_inc(consts, 1)
                for a in (h, xin, scaled, sums):
                    pool.memset(a[:, NT, :], 0.0).then_inc(spare, 1)
                pool.memset(dis[:, NT:NT + 1], 0.0).then_inc(spare, 1)
                pool.memset(w_parts[:, :, 3:4], 0.0).then_inc(spare, 1)
                pool.memset(plus_one[:, :], 1.0).then_inc(spare, 1)
                pool.memset(complete[:, :], NT).then_inc(spare, 1)
                pool.memset(unit_tile[:, 0:1], NT).then_inc(spare, 1)
                pool.iota(iota[:, :], pattern=[[1, STEPS]], base=0, channel_multiplier=0,
                          allow_small_or_imprecise_dtypes=True).then_inc(consts, 1)
                pool.iota(part[:, :], pattern=[[P, EC]], base=0, channel_multiplier=1,
                          allow_small_or_imprecise_dtypes=True).then_inc(consts, 1)
                pool.iota(bounds[:, :], pattern=[[P, NT]], base=0, channel_multiplier=0,
                          allow_small_or_imprecise_dtypes=True).then_inc(consts, 1)
                pool.wait_ge(consts, 11)
                pool.affine_select(out=ident[:, :], in_=ident[:, :], compare_op=ALU.not_equal, fill=1.0,
                                   base=0, pattern=[[-1, P]], channel_multiplier=1).then_inc(consts, 1)
                pool.affine_select(out=below[:, :], in_=below[:, :], compare_op=ALU.is_gt, fill=0.0,
                                   base=0, pattern=[[1, P]], channel_multiplier=-1).then_inc(consts, 1)
                pool.affine_select(out=valid[:, :], in_=valid[:, :], compare_op=ALU.is_gt, fill=0.0,
                                   base=E - (EC - 1) * P * P, pattern=[[-1, P]], channel_multiplier=-P).then_inc(consts, 1)

            @block.vector
            def _(dve):
                n = [0]

                def link(ins):
                    n[0] += 1
                    ins.then_inc(v, 1)
                    dve.wait_ge(v, n[0])

                dve.wait_ge(consts, 14)
                dve.wait_ge(edges_in, 16 * 9)
                link(dve.tensor_copy(e_f[:, 0:2, :, :], e_int[:, :, :, :]))
                for c in range(EC):
                    ins = dve.tensor_scalar(before[:, c, :], bounds[:, :], e_f[:, 0, c, P - 1:P], None, ALU.is_gt)
                ins.then_inc(tiles_cmp, 1)
                ew = e_f[:, 2, :, :]
                link(dve.tensor_scalar(bad_e[:, :, :], ew, 0.0, 0.0, ALU.mult, ALU.not_equal))
                link(dve.copy_predicated(ew, bad_e[:, :, :], zeros[:, :].rearrange("p (c q) -> p c q", c=EC)))
                link(dve.scalar_tensor_tensor(ew, ew, -1.0, ew, ALU.mult, ALU.max))
                link(dve.tensor_scalar(ew, ew, 1e-6, None, ALU.max))
                link(dve.tensor_tensor(e_f[:, 2, EC - 1, :], e_f[:, 2, EC - 1, :], valid[:, :], ALU.mult))
                dve.wait_ge(tiles_sum, 1)
                link(dve.tensor_scalar(first[0:NT, :], ps_b[0:NT, 0:1], part[0:NT, 0:1], None, ALU.add))
                dve.tensor_scalar(begun[0:NT, :], iota[0:NT, :], first[0:NT, 0:1], None, ALU.is_ge).then_inc(first_ready, 1)
                link(dve.memset(ends_f[:, NT - 1:NT], STEPS))
                link(dve.tensor_tensor(ends_f[:, 0:NT - 1], ps_a[:, 1:NT], iota[:, 1:NT], ALU.add))
                link(dve.tensor_scalar(ends_f[:, :], ends_f[:, :], float(RING), None, ALU.add))
                link(dve.tensor_copy(ends[:, 0:NT], ends_f[:, :]))
                dve.wait_ge(node_ps, 1)
                link(dve.tensor_scalar(node_of[:, :], ps_c[:, 0:STEPS], 1.0, None, ALU.subtract))
                link(dve.tensor_tensor(edge_of[:, :], iota[:, :], node_of[:, :], ALU.subtract))
                for c in range(EC):
                    ins = dve.tensor_scalar(pick[:, c, :], edge_of[:, :], part[:, c:c + 1], None, ALU.is_equal)
                ins.then_inc(pick_ready, 1)
                link(dve.tensor_copy(node_i[:, :], node_of[:, :]))
                link(dve.tensor_scalar(slot_off[:, :], node_i[:, :], SLOTS - 1, 9, ALU.bitwise_and, ALU.logical_shift_left))
                link(dve.tensor_scalar(node_next[:, :], node_of[:, :], 1.0, None, ALU.add))
                link(dve.tensor_scalar(node_of4[:, :], node_of[:, :], 4.0, 7.0 * BANK, ALU.mult, ALU.add))
                link(dve.tensor_copy(deg_off[:, :], node_of4[:, :]))
                link(dve.tensor_copy(iota_b[:, :], iota[:, 0:P]))
                dve.wait_ge(spare, 9)
                link(dve.tensor_copy(complete[:, 0:ITERS], node_of[:, 0:STEPS:RING]))
                link(dve.memset(begun_units[:, 0:1], 0.0))
                link(dve.tensor_tensor_scan(begun_units[:, 1:UNITS + 1], plus_one[:, :], complete[:, :], 0.0, ALU.add, ALU.min))
                link(dve.tensor_tensor(taken[:, :], begun_units[:, 1:UNITS + 1], begun_units[:, 0:UNITS], ALU.subtract))
                link(dve.tensor_scalar(unit_f[:, :], begun_units[:, 0:UNITS], -float(NT), None, ALU.add))
                link(dve.tensor_tensor(unit_f[:, :], unit_f[:, :], taken[:, :], ALU.mult))
                link(dve.tensor_scalar(unit_tile[:, 1:UNITS + 1], unit_f[:, :], float(NT), None, ALU.add))
                link(dve.tensor_scalar(unit_wait[:, 0:UNITS], begun_units[:, 1:UNITS + 1], 1.0, None, ALU.add))
                link(dve.tensor_copy(left[:, :], begun_units[:, ITERS + FLUSH - 1:ITERS + FLUSH]))
                dve.wait_ge(x_in, 32)
                for t in range(NT):
                    link(dve.bn_stats(stats[:, :], xin[:, t, :]))
                    ins = dve.bn_aggr(mv[:, t, :], stats[:, :])
                    if t < NT - 1:
                        link(ins)
                ins.then_inc(var_ready, 1)
                dve.wait_ge(step_ps, 1)
                link(dve.scalar_tensor_tensor(rel[:, :], node_of[:, :], -float(P), ps_d[:, 0:STEPS], ALU.mult, ALU.add))
                dve.tensor_copy(src_i[:, :], ps_b[:, 0:STEPS])
                link(dve.tensor_copy(wgt[:, :], ps_a[:, 0:STEPS]))
                for k in range(3):
                    now = w_rest[:, :] if k else wgt[:, :]
                    link(dve.tensor_copy(w_parts[:, :, k:k + 1].rearrange("p s c -> p (s c)"), now))
                    if k < 2:
                        link(dve.tensor_tensor(w_rest[:, :], now, w_parts[:, :, k:k + 1].rearrange("p s c -> p (s c)"),
                                               ALU.subtract))
                dve.wait_ge(std_ready, 1)
                link(dve.reciprocal(rstd[:, :], rstd[:, :]))
                link(dve.scalar_tensor_tensor(shift0[:, :], mv[:, :, 0], -1.0, rstd[:, :], ALU.mult, ALU.mult))

            @block.scalar
            def _(act):
                act.wait_ge(var_ready, 1)
                act.activation(rstd[:, :], mv[:, :, 1], ACT.Sqrt, bias=eps[:, 0:1]).then_inc(std_ready, 1)

            @block.tensor
            def _(pe):
                pe.wait_ge(tiles_cmp, 1)
                for c in range(EC):
                    pe.matmul(ps_a[:, 0:NT], ones[:, :], before[:, c, :], start=(c == 0), stop=(c == EC - 1))
                for c in range(EC):
                    mm = pe.matmul(ps_b[0:NT, 0:1], before[:, c, :], ones[:, 0:1], start=(c == 0), stop=(c == EC - 1))
                mm.then_inc(tiles_sum, 1)
                pe.wait_ge(first_ready, 1)
                pe.matmul(ps_c[:, 0:STEPS], ones[0:NT, :], begun[0:NT, :], start=True, stop=True).then_inc(node_ps, 1)
                pe.wait_ge(pick_ready, 1)
                for k, ps in ((0, ps_d), (1, ps_b), (2, ps_a)):
                    for c in range(EC):
                        mm = pe.matmul(ps[:, 0:STEPS], e_f[:, k, c, :], pick[:, c, :], start=(c == 0), stop=(c == EC - 1))
                mm.then_inc(step_ps, 1)

        hot_free = sem("hot_free")
        hot_ready, deg_ps, deg_ready, dis_ready = (sem(n) for n in ("hot_ready", "deg_ps", "deg_ready", "dis_ready"))
        applied, marked, guarded = sem("applied"), sem("marked"), sem("guarded")
        dv, table_made, table_out = sem("deg_chain"), sem("table_made"), sem("table_out")
        ps_deg = ps_slot[:, 7 * BANK:7 * BANK + 4 * NT]
        ps_mark = [ps_slot[:, k * BANK:(k + 1) * BANK] for k in (4, 5)]
        PAIRS = -(-NT // 2)
        with nc.Block() as block:
            @block.vector
            def _(dve):
                dve.memset(scratch[:, 0:1], 0.0).then_inc(hot_free, RING)
                with dve.Fori(0, ITERS) as i:
                    dve.sem_clear(dv)
                    for g in range(RING // GROUP):
                        dve.wait_ge(hot_free, i * RING + (g + 1) * GROUP)
                        dve.tensor_tensor(w_group[:, g, :, :], w_parts[:, bass.ds(i * RING + g * GROUP, GROUP), :],
                                          zeros_b[:, 0:4 * GROUP].rearrange("p (s c) -> p s c", c=4), ALU.add)
                        dve.tensor_tensor(rel_group[:, g, :], rel[:, bass.ds(i * RING + g * GROUP, GROUP)],
                                          zeros[:, 0:GROUP], ALU.add).then_inc(dv, 1)
                        dve.wait_ge(dv, g + 1)
                        for k in range(GROUP):
                            ins = dve.tensor_scalar(hot[:, g * GROUP + k, :], iota_b[:, :], rel_group[:, g, k:k + 1], None,
                                                    ALU.is_equal)
                        ins.then_inc(hot_ready, 1)
                dve.sem_clear(dv)
                dve.wait_ge(deg_ps, 1)
                dve.tensor_reduce(deg[:, 0:NT], ps_deg.rearrange("p (n c) -> p n c", c=4), AX_X, ALU.add).then_inc(deg_ready, 1)
                for c in range(PAIRS):
                    w = min(2, NT - 2 * c) * D
                    dve.wait_ge(marked, c + 1)
                    dve.copy_predicated(h[:, 2 * c:2 * c + w // D, :].rearrange("p n d -> p (n d)"),
                                        ps_mark[c % 2][:, 0:w].bitcast(I32), zeros[:, 0:w]).then_inc(guarded, 1)
                    if c == 0:
                        dve.wait_ge(dis_ready, 1)
                        dve.reciprocal(dis[:, 0:NT], dis[:, 0:NT]).then_inc(dv, 1)

            @block.tensor
            def _(pe):
                pe.matmul(ps_deg, ones[:, :], zeros_b[:, 0:4 * NT], start=True, stop=False, skip_group_check=True)
                regs = [pe.alloc_register(f"deg_{k}") for k in range(GROUP)]
                with pe.Fori(0, ITERS) as i:
                    for k in range(RING):
                        g, m = k // GROUP, k % GROUP
                        if m == 0:
                            pe.reg_load(regs, deg_off[0:1, bass.ds(i * RING + k, GROUP)])
                            pe.wait_ge(hot_ready, i * (RING // GROUP) + (g + 1))
                        off = pe.snap(regs[m], min_val=0, max_val=4 * NT - 4 + 7 * BANK)
                        mm = pe.matmul(ps_slot[:, bass.ds(off, 4)], hot[:, k, :], w_group[:, g, m, :],
                                       start=False, stop=False, skip_group_check=True)
                        if m == GROUP - 1:
                            mm.then_inc(hot_free, GROUP)
                pe.matmul(ps_slot[:, 6 * BANK:6 * BANK + 2], ones[:, :], zeros_b[:, 0:2], start=True, stop=True).then_inc(deg_ps, 1)

            @block.scalar
            def _(act):
                for t in range(NT):
                    act.activation(h[:, t, :], xin[:, t, :], ACT.Identity, bias=shift0[:, t:t + 1],
                                   scale=rstd[:, t:t + 1]).then_inc(applied, 1)

                def mark(c):
                    w = min(2, NT - 2 * c) * D
                    act.activation(ps_mark[c % 2][:, 0:w], h[:, 2 * c:2 * c + w // D, :].rearrange("p n d -> p (n d)"),
                                   ACT.Identity, bias=zeros[:, 0:1], scale=0.0).then_inc(marked, 1)

                act.wait_ge(applied, NT)
                mark(0)
                mark(1)
                act.wait_ge(deg_ready, 1)
                act.activation(dis[:, 0:NT], deg[:, :], ACT.Sqrt, bias=ones_f[:, 0:1]).then_inc(dis_ready, 1)
                act.wait_ge(dv, 1)
                for c in range(PAIRS):
                    act.wait_ge(guarded, c + 1)
                    for t in range(2 * c, min(NT, 2 * c + 2)):
                        act.activation(scaled[:, t, :], h[:, t, :], ACT.Copy, scale=dis[:, t:t + 1]).then_inc(table_made, 1)
                    if c + 2 < PAIRS:
                        mark(c + 2)

            @block.sync
            def _(sp):
                for c in range(NT // UN):
                    sp.wait_ge(table_made, UN * (c + 1))
                    sp.dma_start(tables[0][UN * P * c:UN * P * (c + 1), :].rearrange("(n p) d -> p n d", p=P),
                                 scaled[:, UN * c:UN * (c + 1), :]).then_inc(table_out, 16)
                sp.wait_ge(table_out, 16 * (NT // UN))

        setup_mem.close()
        rows = sb("rows", [P, RING, D])
        smat = sb("smat", [P, RING, P])
        u = sb("u", [P, D])
        ut = sb("ut", [P, KD, P])
        y = sb("y", [P, D])
        z = sb("z", [P, D])
        x1s = sb("x1s", [P, D])
        ps_t, ps_y, ps_bad = (ps_slot[:, k * BANK:k * BANK + D] for k in (4, 5, 6))

        def layer_pass(q):
            bias, gain, shift = vec[:, 3 * q, :], vec[:, 3 * q + 1, :], vec[:, 3 * q + 2, :]
            ring_free, s_ready, slot_free, evac, u_ready, turned, ut_ready, y_ps, tile_done, stored, v = (
                sem(f"{n}_layer{q}") for n in ("ring_free", "s_ready", "slot_free", "evac", "u_ready", "turned", "ut_ready",
                                         "y_ps", "tile_done", "stored", "unit_chain"))
            landed = [sem(f"landed{q}_{k}") for k in range(RING)]
            target = x1_dram if q else tables[1]

            with nc.Block() as block:
                @block.gpsimd
                def _(pool):
                    for s in range(STEPS):
                        k = s % RING
                        if k % GROUP == 0 and s >= RING:
                            pool.wait_ge(ring_free, s + GROUP)
                        pool.indirect_dma_start(
                            rows[:, k, :], None, tables[q][0:NT * P, :],
                            bass.IndirectOffsetOnAxis(ap=src_i[:, s:s + 1].bitcast(U32), axis=0)).then_inc(landed[k], 16)

                @block.tensor
                def _(pe):
                    if q == 0:
                        for b in range(SLOTS):
                            mm = pe.matmul(ps_slot[:, SLOT * b:SLOT * b + D], ones[:, :], zeros_b[:, :],
                                           start=True, stop=False, skip_group_check=True)
                    pe.matmul(ps_y, ones[:, :], zeros_b[:, :], start=True, stop=True).then_inc(y_ps, 1)
                    regs = [pe.alloc_register(f"slot{q}_{k}") for k in range(GROUP)]
                    last = [pe.alloc_register(f"last{q}_{k}") for k in range(2)]

                    def steps(i, g):
                        pe.reg_load(regs, slot_off[0:1, bass.ds(i * RING + g * GROUP, GROUP)])
                        for k in range(2):
                            pe.reg_load(last[k], node_next[0:1, bass.ds(i * RING + (g * GROUP + SLOTS * (k + 1) - 1), 1)])
                        for k in range(GROUP):
                            if k % SLOTS == 0:
                                pe.wait_ge(slot_free, pe.snap(last[k // SLOTS], min_val=1, max_val=NT))
                            b = g * GROUP + k
                            pe.wait_ge(s_ready, i * RING + (b + 1))
                            pe.wait_ge(landed[b], i * 16 + 16)
                            off = pe.snap(regs[k], min_val=0, max_val=(SLOTS - 1) * SLOT)
                            pe.matmul(ps_slot[:, bass.ds(off, D)], smat[:, b, :], rows[:, b, :],
                                      start=False, stop=False, skip_group_check=True).then_inc(ring_free, 1)

                    def turn_u(i):
                        pe.wait_ge(u_ready, i + 1)
                        for c in range(KD):
                            mm = pe.transpose(ps_t[:, c * P:(c + 1) * P], u[:, c * P:(c + 1) * P], ident[:, :])
                        mm.then_inc(turned, 1)

                    def product(i):
                        pe.wait_ge(ut_ready, i + 1)
                        for c in range(KD):
                            mm = pe.matmul(ps_y, ut[:, c, :], wmat[:, q, c, :], start=(c == 0), stop=(c == KD - 1))
                        mm.then_inc(y_ps, 1)

                    with pe.Fori(0, ITERS) as i:
                        steps(i, 0)
                        turn_u(i)
                        steps(i, 1)
                        product(i)
                    with pe.Fori(ITERS, ITERS + FLUSH) as i:
                        turn_u(i)
                        product(i)
                    more = pe.alloc_register(f"more_pe{q}")
                    pe.reg_load(more, left[0:1, 0:1])
                    with pe.If(pe.snap(more, min_val=0, max_val=NT) < NT):
                        with pe.Fori(ITERS + FLUSH, UNITS) as i:
                            turn_u(i)
                            product(i)

                @block.scalar
                def _(act):
                    regs = [act.alloc_register(f"end{q}_{k}") for k in range(GROUP)]
                    for t in range(NT):
                        if t % GROUP == 0:
                            m = min(GROUP, NT - t)
                            act.reg_load(regs[0:m], ends[0:1, t:t + m])
                        s = (t % SLOTS) * SLOT
                        act.wait_ge(ring_free, act.snap(regs[t % GROUP], min_val=RING, max_val=RING + STEPS))
                        act.activation(sums[:, t, :], ps_slot[:, s:s + D], ACT.Copy).then_inc(evac, 1)
                        act.wait_ge(evac, t + 2)
                        act.activation(ps_slot[:, s:s + D], zeros[:, 0:D], ACT.Copy).then_inc(slot_free, 1)

                @block.vector
                def _(dve):
                    n = [0]

                    def link(ins):
                        n[0] += 1
                        ins.then_inc(v, 1)
                        dve.wait_ge(v, n[0])

                    def tile(a, t):
                        return a[:, bass.ds(t, 1), :].rearrange("p a d -> p (a d)")

                    def guard(a):
                        link(dve.tensor_scalar(ps_bad, a, 0.0, 0.0, ALU.mult, ALU.not_equal))
                        link(dve.copy_predicated(a, ps_bad.bitcast(I32), zeros[:, 0:D]))

                    def norm():
                        var, w, r, a, fin = (small[:, k:k + 1] for k in (1, 2, 3, 4, 5))
                        dve.tensor_scalar(fin, var, 3.0e38, None, ALU.is_le)
                        link(dve.tensor_scalar(w, var, EPS, 3.0e38, ALU.add, ALU.min))
                        link(dve.tensor_scalar(r.bitcast(I32), w.bitcast(I32), -0.5, 1597463007.0, ALU.mult, ALU.add))
                        for less in (3.0, 12.0, 768.0):
                            link(dve.scalar_tensor_tensor(a, r, w, r, ALU.mult, ALU.mult))
                            link(dve.scalar_tensor_tensor(r, a, less, r, ALU.subtract, ALU.mult))
                        link(dve.tensor_scalar(a, r, -1.0 / 8192.0, fin, ALU.mult, ALU.mult))
                        return a

                    def build(i, g):
                        dve.wait_ge(ring_free, i * RING + (g + 1) * GROUP)
                        for k in range(g * GROUP, (g + 1) * GROUP):
                            dve.tensor_scalar(smat[:, k, :], iota[:, 0:P], rel[:, bass.ds(i * RING + k, 1)],
                                              wgt[:, bass.ds(i * RING + k, 1)], ALU.is_equal, ALU.mult).then_inc(s_ready, 1)

                    unit_regs = [dve.alloc_register(f"unit{q}_{k}") for k in range(2)]
                    wait_reg = dve.alloc_register(f"unit_wait{q}")

                    def unit(i):
                        dve.reg_load(unit_regs, unit_tile[0:1, bass.ds(i, 2)])
                        dve.reg_load(wait_reg, unit_wait[0:1, bass.ds(i, 1)])
                        prev, cur = (dve.snap(r, min_val=0, max_val=NT) for r in unit_regs)
                        dve.sem_clear(v)
                        n[0] = 0
                        dve.wait_ge(y_ps, i + 1)
                        dve.scalar_tensor_tensor(y[:, :], ps_y, dis[:, bass.ds(prev, 1)], bias, ALU.mult, ALU.add).then_inc(v, 1)
                        n[0] += 1
                        dve.wait_ge(evac, dve.snap(wait_reg, min_val=1, max_val=NT + 1))
                        dve.tensor_tensor(u[:, :], tile(sums, cur), tile(scaled, cur), ALU.add).then_inc(u_ready, 1)
                        dve.wait_ge(v, n[0])
                        guard(y[:, :])
                        link(dve.bn_stats(stats[:, :], y[:, :]))
                        link(dve.bn_aggr(small[:, 0:2], stats[:, :]))
                        r = norm()
                        link(dve.scalar_tensor_tensor(y[:, :], y[:, :], small[:, 0:1], gain, ALU.subtract, ALU.mult))
                        link(dve.scalar_tensor_tensor(y[:, :], y[:, :], r, shift, ALU.mult, ALU.add))
                        guard(y[:, :])
                        link(dve.scalar_tensor_tensor(z[:, :], y[:, :], 0.0, tile(h, prev), ALU.max, ALU.add))
                        guard(z[:, :])
                        dve.wait_ge(stored, i * 16 + 16)
                        if q == 0:
                            dve.tensor_scalar(tile(scaled, prev), z[:, :], dis[:, bass.ds(prev, 1)], None,
                                              ALU.mult).then_inc(tile_done, 1)
                            dve.tensor_copy(tile(h, prev), z[:, :])
                        else:
                            dve.tensor_tensor(x1s[:, :], z[:, :], tile(xin, prev), ALU.add).then_inc(tile_done, 1)
                            dve.wait_ge(tile_done, i + 1)
                            link(dve.bn_stats(stats[:, :], x1s[:, :]))
                            link(dve.bn_aggr(small[:, 0:2], stats[:, :]))
                            r = norm()
                            dve.tensor_scalar(tile(x2, prev), x1s[:, :], small[:, 0:1], r, ALU.subtract, ALU.mult)
                        dve.wait_ge(turned, i + 1)
                        dve.tensor_copy(ut[:, :, :].rearrange("p c q -> p (c q)"), ps_t).then_inc(ut_ready, 1)

                    for k, s in enumerate((ring_free, slot_free, evac, stored)):
                        dve.memset(scratch[:, k:k + 1], 0.0).then_inc(s, (RING, SLOTS, 1, 16)[k])
                    with dve.Fori(0, ITERS) as i:
                        build(i, 0)
                        build(i, 1)
                        unit(i)
                    with dve.Fori(ITERS, ITERS + FLUSH) as i:
                        unit(i)
                    more = dve.alloc_register(f"more_dve{q}")
                    dve.reg_load(more, left[0:1, 0:1])
                    with dve.If(dve.snap(more, min_val=0, max_val=NT) < NT):
                        with dve.Fori(ITERS + FLUSH, UNITS) as i:
                            unit(i)

                @block.sync
                def _(sp):
                    reg = sp.alloc_register(f"unit_sp{q}")

                    def store(i):
                        sp.reg_load(reg, unit_tile[0:1, bass.ds(i, 1)])
                        t = sp.snap(reg, min_val=0, max_val=NT)
                        sp.wait_ge(tile_done, i + 1)
                        sp.dma_start(target[bass.ds(t * P, P), :], x1s[:, :] if q else
                                     scaled[:, bass.ds(t, 1), :].rearrange("p a d -> p (a d)")).then_inc(stored, 16)

                    with sp.Fori(0, ITERS + FLUSH) as i:
                        store(i)
                    sp.wait_ge(stored, 16 * (ITERS + FLUSH + 1))
                    more = sp.alloc_register(f"more_sp{q}")
                    sp.reg_load(more, left[0:1, 0:1])
                    with sp.If(sp.snap(more, min_val=0, max_val=NT) < NT):
                        with sp.Fori(ITERS + FLUSH, UNITS) as i:
                            store(i)
                        sp.wait_ge(stored, 16 * (UNITS + 1))

        layer_pass(0)
        layer_pass(1)

        x2_turned, x2t_ready, logit_ps, logits_out = (
            sem(n) for n in ("x2_turned", "x2t_ready", "logit_ps", "logits_out"))
        x2t = sb("x2t", [P, 2, KD, P])
        ps_x = [ps_slot[:, k * BANK:k * BANK + D] for k in range(2)]
        ps_l = [ps_slot[:, k * BANK:k * BANK + EXPERTS] for k in (2, 3)]
        with nc.Block() as block:
            @block.tensor
            def _(pe):
                def turn_x2(t):
                    if t >= 2:
                        pe.wait_ge(x2t_ready, t - 1)
                    for c in range(KD):
                        mm = pe.transpose(ps_x[t % 2][:, c * P:(c + 1) * P], x2[:, t, c * P:(c + 1) * P], ident[:, :])
                    mm.then_inc(x2_turned, 1)

                turn_x2(0)
                for t in range(NT):
                    if t + 1 < NT:
                        turn_x2(t + 1)
                    pe.wait_ge(x2t_ready, t + 1)
                    if t >= 2:
                        pe.wait_ge(logits_out, t - 1)
                    for c in range(KD):
                        mm = pe.matmul(ps_l[t % 2], x2t[:, t % 2, c, :], gwt[:, c, :], start=(c == 0), stop=(c == KD - 1))
                    mm.then_inc(logit_ps, 1)

            @block.scalar
            def _(act):
                for t in range(NT):
                    act.wait_ge(x2_turned, t + 1)
                    if t >= 2:
                        act.wait_ge(logit_ps, t - 1)
                    act.activation(x2t[:, t % 2, :, :].rearrange("p c q -> p (c q)"), ps_x[t % 2], ACT.Copy).then_inc(x2t_ready, 1)

            @block.vector
            def _(dve):
                for t in range(NT):
                    dve.wait_ge(logit_ps, t + 1)
                    dve.tensor_tensor(logits[:, t, :], ps_l[t % 2], gbias[:, :], ALU.add).then_inc(logits_out, 1)


def route(nc, sem, g, logits, sb):
    ones, below = g["ones"], g["below"]
    slot_id, top_w, w_off, ps_a, ps_b = g["slot_id"], g["top_w"], g["w_off"], g["ps_a"], g["ps_b"]
    one = [sb(f"one{k}", [P, NT, EXPERTS]) for k in range(2)]
    cand = sb("cand", [P, NT, EXPERTS])
    work = sb("work", [P, NT, EXPERTS])
    both = sb("both", [P, NT, EXPERTS], BF16)
    best = sb("best", [P, 2, NT])
    which = sb("which", [P, 2, NT])
    eids = sb("eids", [P, EXPERTS])
    live = sb("live", [P, NT])
    carry = sb("carry", [P, NT + 1, EXPERTS])
    count_i = sb("count_i", [P, EXPERTS], I32)
    nblk = sb("nblk", [P, 2, EXPERTS])
    blk_end = sb("blk_end", [P, EXPERTS])
    blk_start = sb("blk_start", [P, EXPERTS])
    bnum = sb("bnum", [P, BLOCKS])
    over = sb("over", [P, BLOCKS, EXPERTS])
    eid_b = sb("eid_b", [P, BLOCKS])
    slot_f = sb("slot_f", [P, 2, NT])
    gap = sb("gap", [P, NT])
    eg = sb("eg", [P, NT])
    neg = sb("neg", [P, NT, EXPERTS])
    flag = sb("flag", [P, NT, EXPERTS], I32)
    rc, ready, counted, v, ex = (sem(n) for n in ("route_consts", "route_onehot", "route_counted", "route_chain", "route_exp"))
    gapped = sem("route_gap")
    row = [P, NT, EXPERTS]

    def over_e(a):
        return a.rearrange("p (n e) -> p n e", e=1).to_broadcast(row)

    def over_n(a):
        return a.rearrange("p (n e) -> p n e", n=1).to_broadcast(row)

    with nc.Block() as block:
        @block.gpsimd
        def _(pool):
            pool.iota(eids[:, :], pattern=[[1, EXPERTS]], base=0, channel_multiplier=0,
                      allow_small_or_imprecise_dtypes=True).then_inc(rc, 1)
            pool.iota(bnum[:, :], pattern=[[1, BLOCKS]], base=0, channel_multiplier=0,
                      allow_small_or_imprecise_dtypes=True).then_inc(rc, 1)
            pool.memset(neg[:, :, :], -3.4e38).then_inc(rc, 1)
            pool.memset(live[:, :], 1.0).then_inc(rc, 1)
            pool.wait_ge(rc, 4)
            pool.affine_select(out=live[:, :], in_=live[:, :], compare_op=ALU.is_gt, fill=0.0, base=N,
                               pattern=[[-P, NT]], channel_multiplier=-1).then_inc(rc, 1)

        @block.tensor
        def _(pe):
            pe.wait_ge(ready, 1)
            both2 = both[:, :, :].rearrange("p n e -> p (n e)")
            pe.matmul(ps_a[:, 0:NT * EXPERTS], below[:, :], both2, start=True, stop=True)
            pe.matmul(ps_b[:, 0:NT * EXPERTS], ones[:, :], both2, start=True, stop=True).then_inc(counted, 1)

        @block.scalar
        def _(act):
            act.wait_ge(gapped, 1)
            act.activation(eg[:, :], gap[:, :], ACT.Exp).then_inc(ex, 1)

        @block.vector
        def _(dve):
            n = [0]

            def link(ins):
                n[0] += 1
                ins.then_inc(v, 1)
                dve.wait_ge(v, n[0])

            dve.wait_ge(rc, 5)
            for k in range(2):
                link(dve.tensor_reduce(best[:, k, :], logits[:, :, :], AX_X, ALU.max))
                link(dve.tensor_tensor(cand[:, :, :], logits[:, :, :], over_e(best[:, k, :]), ALU.is_equal))
                link(dve.tensor_scalar(cand[:, :, :], cand[:, :, :], -float(EXPERTS), float(EXPERTS), ALU.mult, ALU.add))
                link(dve.tensor_tensor(cand[:, :, :], cand[:, :, :], over_n(eids[:, :]), ALU.add))
                link(dve.tensor_reduce(which[:, k, :], cand[:, :, :], AX_X, ALU.min))
                link(dve.tensor_scalar(which[:, k, :], which[:, k, :], EXPERTS - 1.0, None, ALU.min))
                link(dve.tensor_tensor(one[k][:, :, :], over_n(eids[:, :]), over_e(which[:, k, :]), ALU.is_equal))
                if k == 0:
                    link(dve.tensor_copy(flag[:, :, :], one[0][:, :, :]))
                    link(dve.copy_predicated(logits[:, :, :], flag[:, :, :], neg[:, :, :]))
            dve.tensor_tensor(gap[:, :], best[:, 1, :], best[:, 0, :], ALU.subtract).then_inc(gapped, 1)
            link(dve.tensor_tensor(work[:, :, :], one[0][:, :, :], one[1][:, :, :], ALU.add))
            dve.tensor_tensor(both[:, :, :], work[:, :, :], over_e(live[:, :]), ALU.mult).then_inc(ready, 1)
            dve.wait_ge(ex, 1)
            link(dve.tensor_scalar(top_w[:, 0, :], eg[:, :], 1.0, None, ALU.add))
            link(dve.reciprocal(top_w[:, 0, :], top_w[:, 0, :]))
            link(dve.tensor_tensor(top_w[:, 1, :], top_w[:, 0, :], eg[:, :], ALU.mult))
            link(dve.memset(carry[:, 0, :], 0.0))
            dve.wait_ge(counted, 1)
            for t in range(NT):
                link(dve.tensor_tensor(carry[:, t + 1, :], carry[:, t, :], ps_b[:, t * EXPERTS:(t + 1) * EXPERTS], ALU.add))
            link(dve.tensor_scalar(nblk[:, 0, :], carry[:, NT, :], P - 1.0, None, ALU.add))
            link(dve.tensor_copy(count_i[:, :], nblk[:, 0, :]))
            link(dve.tensor_scalar(count_i[:, :], count_i[:, :], 7, None, ALU.logical_shift_right))
            link(dve.tensor_copy(nblk[:, 1, :], count_i[:, :]))
            link(dve.tensor_copy(blk_end[:, :], nblk[:, 1, :]))
            for e in range(1, EXPERTS):
                link(dve.tensor_tensor(blk_end[:, e:e + 1], blk_end[:, e:e + 1], blk_end[:, e - 1:e], ALU.add))
            link(dve.tensor_tensor(blk_start[:, :], blk_end[:, :], nblk[:, 1, :], ALU.subtract))
            link(dve.tensor_scalar(blk_start[:, :], blk_start[:, :], float(P), None, ALU.mult))
            link(dve.tensor_tensor(work[:, :, :], carry[:, 0:NT, :],
                                   ps_a[:, 0:NT * EXPERTS].rearrange("p (n e) -> p n e", e=EXPERTS), ALU.add))
            link(dve.tensor_tensor(work[:, :, :], work[:, :, :], over_n(blk_start[:, :]), ALU.add))
            for k in range(2):
                link(dve.tensor_tensor(cand[:, :, :], work[:, :, :], one[k][:, :, :], ALU.mult))
                link(dve.tensor_reduce(slot_f[:, k, :], cand[:, :, :], AX_X, ALU.add))
            link(dve.tensor_copy(slot_id[:, :, :], slot_f[:, :, :]))
            wide = [P, BLOCKS, EXPERTS]
            link(dve.tensor_tensor(over[:, :, :], bnum[:, :].rearrange("p (b e) -> p b e", e=1).to_broadcast(wide),
                                   blk_end[:, :].rearrange("p (b e) -> p b e", b=1).to_broadcast(wide), ALU.is_ge))
            link(dve.tensor_reduce(eid_b[:, :], over[:, :, :], AX_X, ALU.add))
            link(dve.tensor_scalar(eid_b[:, :], eid_b[:, :], EXPERTS - 1.0, None, ALU.min))
            link(dve.tensor_copy(w_off[:, :], eid_b[:, :]))


def experts(nc, sem, g):
    ident, x2, slot_id, top_w, w_off = g["ident"], g["x2"], g["slot_id"], g["top_w"], g["w_off"]
    rows_in, rows_out, x1_dram, out = g["rows_in"], g["rows_out"], g["x1_dram"], g["out"]
    ps_slot, ps_a, ps_b, ps_c, ps_d = g["ps_slot"], g["ps_a"], g["ps_b"], g["ps_c"], g["ps_d"]
    ring = 4
    with ExitStack() as ctx:
        def sb(name, shape, dt=F32):
            return ctx.enter_context(nc.sbuf_tensor(name, shape, dt))

        with ExitStack() as inner:
            def sbi(name, shape, dt=F32):
                return inner.enter_context(nc.sbuf_tensor(name, shape, dt))
            w1 = sbi("w1", [P, EXPERTS * KD * F])
            w2 = sbi("w2", [P, EXPERTS * KF * D])
            b1r = sbi("b1r", [EXPERTS * KF, P])
            b1t = sbi("b1t", [P, EXPERTS * KF])
            b2b = sbi("b2b", [P, EXPERTS * D])
            xb = sbi("xb", [P, ring, D])
            xt = sbi("xt", [P, 2, KD, P])
            hid = sbi("hid", [P, 2, F])
            hidt = sbi("hidt", [P, 2, KF, P])
            yb = sbi("yb", [P, 2, D])

            scattered, w_in, b_in = sem("scattered"), sem("w_in"), sem("b_in")
            b1_ps, b1_ready = sem("b1_ps"), sem("b1_ready")
            xb_in = [sem(f"xb_in{k}") for k in range(ring)]
            x_turned, xt_ready, h_ps, hid_ready, h_turned, hidt_ready, out_ps, y_ready = (
                sem(n) for n in ("x_turned", "xt_ready", "h_ps", "hid_ready", "h_turned", "hidt_ready", "out_ps", "y_ready"))
            y_out = [sem(f"y_out{k}") for k in range(2)]
            B4 = 4
            with nc.Block() as block:
                @block.gpsimd
                def _(pool):
                    pool.wait_ge(g["zeroed_rows"], 16 * (ROWS // P // 2))
                    for t in range(NT):
                        m = P if t < NT - 1 else LAST
                        for k in range(2):
                            pool.indirect_dma_start(
                                rows_in[:, :], bass.IndirectOffsetOnAxis(ap=slot_id[0:m, k, t:t + 1].bitcast(U32), axis=0),
                                x2[0:m, t, :], None).then_inc(scattered, 16)
                    pool.wait_ge(scattered, 32 * NT)

                @block.sync
                def _(sp):
                    for e in range(EXPERTS):
                        sp.dma_start(w1[:, e * KD * F:(e + 1) * KD * F].rearrange("p (k f) -> p k f", k=KD),
                                     g["ew1"][e].rearrange("(k p) f -> p k f", p=P)).then_inc(w_in, 16)
                    sp.dma_start(b1r[:, :], g["eb1"].rearrange("e (c p) -> (e c) p", p=P)).then_inc(b_in, 16)
                    sp.dma_start(b2b[:, :], g["eb2"].rearrange("(a e) d -> a (e d)", a=1).to_broadcast([P, EXPERTS * D])).then_inc(b_in, 16)
                    for e in range(EXPERTS):
                        sp.dma_start(w2[:, e * KF * D:(e + 1) * KF * D].rearrange("p (k f) -> p k f", k=KF),
                                     g["ew2"][e].rearrange("(k p) f -> p k f", p=P)).then_inc(w_in, 16)
                    sp.wait_ge(scattered, 32 * NT)

                    def load(b, k):
                        sp.dma_start(xb[:, k, :], rows_in[bass.ds(b * P, P), :]).then_inc(xb_in[k], 16)

                    def store(b, k):
                        sp.wait_ge(y_ready, b + 3)
                        sp.dma_start(rows_out[bass.ds(b * P, P), :], yb[:, k % 2, :]).then_inc(y_out[k % 2], 16)

                    for k in range(ring):
                        load(k, k)
                    with sp.Fori(0, BLOCKS // ring - 1) as i:
                        for k in range(ring):
                            sp.wait_ge(x_turned, i * ring + (k + 1))
                            load(i * ring + (k + ring), k)
                            store(i * ring + k, k)
                    for k in range(ring):
                        store(BLOCKS - ring + k, k)
                    for k in range(2):
                        sp.wait_ge(y_out[k], 16 * (BLOCKS // 2 + 1))

                px, ph, pt, py = ([ps_slot[:, (2 * j + k) * BANK:(2 * j + k) * BANK + w] for k in range(2)]
                                  for j, w in enumerate((D, F, F, D)))
                pb = ps_slot[:, 0:EXPERTS * KF]

                @block.tensor
                def _(pe):
                    pe.wait_ge(b_in, 32)
                    pe.transpose(pb, b1r[:, :], ident[0:EXPERTS * KF, 0:EXPERTS * KF]).then_inc(b1_ps, 1)
                    pe.wait_ge(b1_ready, 1)
                    regs = [pe.alloc_register(f"expert{k}") for k in range(ring + 2)]

                    def turn_x(b, q, loads):
                        pe.wait_ge(xb_in[q], loads * 16)
                        for c in range(KD):
                            mm = pe.transpose(px[q % 2][:, c * P:(c + 1) * P], xb[:, q, c * P:(c + 1) * P], ident[:, :])
                        mm.then_inc(x_turned, 1)

                    def up(b, q, e):
                        pe.wait_ge(xt_ready, b + 1)
                        for c in range(KD):
                            mm = pe.matmul(ph[q % 2], xt[:, q % 2, c, :], w1[:, bass.ds(e * (KD * F) + c * F, F)],
                                           start=(c == 0), stop=(c == KD - 1))
                        mm.then_inc(h_ps, 1)

                    def turn_h(b, q):
                        pe.wait_ge(hid_ready, b + 1)
                        for c in range(KF):
                            mm = pe.transpose(pt[q % 2][:, c * P:(c + 1) * P], hid[:, q % 2, c * P:(c + 1) * P], ident[:, :])
                        mm.then_inc(h_turned, 1)

                    def down(b, q, e):
                        pe.wait_ge(hidt_ready, b + 1)
                        pe.wait_ge(y_ready, b + 1)
                        for c in range(KF):
                            mm = pe.matmul(py[q % 2], hidt[:, q % 2, c, :], w2[:, bass.ds(e * (KF * D) + c * D, D)],
                                           start=(c == 0), stop=(c == KF - 1))
                        mm.then_inc(out_ps, 1)

                    def expert(k):
                        return pe.snap(regs[k], min_val=0, max_val=EXPERTS - 1)

                    turn_x(0, 0, 1)
                    turn_x(1, 1, 1)
                    pe.wait_ge(w_in, 32 * EXPERTS)
                    pe.reg_load(regs[0:3], w_off[0:1, 0:3])
                    first = [expert(k) for k in range(3)]
                    up(0, 0, first[0])
                    up(1, 1, first[1])
                    turn_h(0, 0)
                    turn_x(2, 2, 1)
                    up(2, 2, first[2])
                    turn_h(1, 1)
                    down(0, 0, first[0])
                    turn_x(3, 3, 1)
                    with pe.Fori(0, BLOCKS // ring - 1) as i:
                        pe.reg_load(regs, w_off[0:1, bass.ds(i * ring + 1, ring + 2)])
                        for k in range(ring):
                            b = i * ring + (2 + k)
                            up(b + 1, (3 + k) % ring, expert(k + 2))
                            turn_h(b, (2 + k) % ring)
                            down(b - 1, (1 + k) % ring, expert(k))
                            turn_x(b + 2, k, i + 2)
                    pe.reg_load(regs[0:3], w_off[0:1, BLOCKS - 3:BLOCKS])
                    last = [expert(k) for k in range(3)]
                    b = BLOCKS - 2
                    up(b + 1, (b + 1) % ring, last[2])
                    turn_h(b, b % ring)
                    down(b - 1, (b - 1) % ring, last[0])
                    turn_h(b + 1, (b + 1) % ring)
                    down(b, b % ring, last[1])
                    down(b + 1, (b + 1) % ring, last[2])

                @block.scalar
                def _(act):
                    act.wait_ge(b1_ps, 1)
                    act.activation(b1t[:, :], pb, ACT.Copy).then_inc(b1_ready, 1)

                    def copy_x(b, s):
                        act.wait_ge(x_turned, b + 1)
                        act.activation(xt[:, s, :, :].rearrange("p c q -> p (c q)"), px[s], ACT.Copy).then_inc(xt_ready, 1)

                    def copy_h(b, s):
                        act.wait_ge(h_ps, b + 1)
                        act.activation(hid[:, s, :], ph[s], ACT.Copy).then_inc(hid_ready, 1)

                    copy_x(0, 0)
                    copy_x(1, 1)
                    copy_h(0, 0)
                    with act.Fori(0, BLOCKS // 2 - 1) as i:
                        for k in range(2):
                            copy_h(i * 2 + (1 + k), (1 + k) % 2)
                            copy_x(i * 2 + (2 + k), k)
                    copy_h(BLOCKS - 1, 1)

                @block.vector
                def _(dve):
                    dve.memset(yb[:, 0, 0:1], 0.0).then_inc(y_ready, 2)
                    dve.memset(yb[:, 0, 1:2], 0.0).then_inc(y_out[0], 16)
                    dve.memset(yb[:, 0, 2:3], 0.0).then_inc(y_out[1], 16)
                    dve.wait_ge(y_out[1], 16)
                    dve.wait_ge(b_in, 32)
                    dve.wait_ge(b1_ready, 1)
                    regs = [dve.alloc_register(f"expert_v{k}") for k in range(3)]

                    def relu_h(b, s, e):
                        dve.wait_ge(h_turned, b + 1)
                        for c in range(KF):
                            ins = dve.tensor_scalar(hidt[:, s, c, :], pt[s][:, c * P:(c + 1) * P],
                                                    b1t[:, bass.ds(e * KF + c, 1)], 0.0, ALU.add, ALU.max)
                        ins.then_inc(hidt_ready, 1)

                    def add_b2(b, s, e, uses):
                        dve.wait_ge(y_out[s], uses * 16)
                        dve.wait_ge(out_ps, b + 1)
                        dve.tensor_tensor(yb[:, s, :], py[s], b2b[:, bass.ds(e * D, D)], ALU.add).then_inc(y_ready, 1)

                    def expert(k):
                        return dve.snap(regs[k], min_val=0, max_val=EXPERTS - 1)

                    dve.reg_load(regs[0:2], w_off[0:1, 0:2])
                    relu_h(0, 0, expert(0))
                    relu_h(1, 1, expert(1))
                    add_b2(0, 0, expert(0), 1)
                    with dve.Fori(0, BLOCKS // 2 - 1) as i:
                        dve.reg_load(regs, w_off[0:1, bass.ds(i * 2 + 1, 3)])
                        for k in range(2):
                            relu_h(i * 2 + (2 + k), k, expert(k + 1))
                            add_b2(i * 2 + (1 + k), (1 + k) % 2, expert(k), i + (1 + k))
                    dve.reg_load(regs[0:1], w_off[0:1, BLOCKS - 1:BLOCKS])
                    add_b2(BLOCKS - 1, 1, expert(0), BLOCKS // 2)

        combine(nc, sem, g, sb)


def combine(nc, sem, g, sb):
    x2, slot_id, top_w, rows_out, x1_dram, out = (g[n] for n in ("x2", "slot_id", "top_w", "rows_out", "x1_dram", "out"))
    ya = sb("ya", [P, UN, 2, D])
    x1t = sb("x1t", [P, UN, D])
    y_sum = sb("y_sum", [P, UN, D])
    res = sb("res", [P, UN, D])
    gam = sb("gam", [P, D])
    bet = sb("bet", [P, D])
    stats = sb("stats2", [P, 6])
    mv = sb("mv2", [P, 2, 2])
    std = sb("std2", [P, 2])
    rstd = sb("rstd2", [P, 2])
    fetched = [sem(f"fetched{k}") for k in range(UN)]
    x1_in = [sem(f"x1_in{k}") for k in range(UN)]
    stored = [sem(f"stored{k}") for k in range(UN)]
    var_ready, std_ready = sem("var_ready2"), sem("std_ready2")
    padded, gb_in, cv, done = sem("padded2"), sem("gb_in"), sem("combine_chain"), sem("combined")
    with nc.Block() as block:
        @block.gpsimd
        def _(pool):
            pool.memset(ya[:, UN - 1, :, :], 0.0).then_inc(padded, 1)
            pool.wait_ge(padded, 1)
            for t in range(NT):
                m = P if t < NT - 1 else LAST
                if t >= UN:
                    pool.wait_ge(done, t - UN + 1)
                for k in range(2):
                    pool.indirect_dma_start(
                        ya[0:m, t % UN, k, :], None, rows_out[:, :],
                        bass.IndirectOffsetOnAxis(ap=slot_id[0:m, k, t:t + 1].bitcast(U32), axis=0)
                    ).then_inc(fetched[t % UN], 16)

        @block.sync
        def _(sp):
            sp.dma_start(gam[:, :], g["gamma"].rearrange("(a d) -> a d", a=1).to_broadcast([P, D])).then_inc(gb_in, 16)
            sp.dma_start(bet[:, :], g["beta"].rearrange("(a d) -> a d", a=1).to_broadcast([P, D])).then_inc(gb_in, 16)
            for t in range(NT + UN - 1):
                if t < NT:
                    if t >= UN:
                        sp.wait_ge(done, t - UN + 1)
                    sp.dma_start(x1t[:, t % UN, :], x1_dram[t * P:(t + 1) * P, :]).then_inc(x1_in[t % UN], 16)
                d = t - (UN - 1)
                if d >= 0:
                    m = P if d < NT - 1 else LAST
                    sp.wait_ge(done, d + 1)
                    sp.dma_start(out[d * P:d * P + m, :], res[0:m, d % UN, :]).then_inc(stored[d % UN], 16)
            for k in range(UN):
                sp.wait_ge(stored[k], 16 * (NT // UN))

        @block.scalar
        def _(act):
            for t in range(NT):
                act.wait_ge(var_ready, t + 1)
                act.activation(std[:, t % 2:t % 2 + 1], mv[:, t % 2, 1:2], ACT.Sqrt, bias=g["eps"][:, 0:1]).then_inc(std_ready, 1)

        @block.vector
        def _(dve):
            dve.wait_ge(gb_in, 32)
            n = [0]

            def link(ins):
                n[0] += 1
                ins.then_inc(cv, 1)
                dve.wait_ge(cv, n[0])

            for t in range(NT + 1):
                k, p = t % UN, (t - 1) % UN
                if t < NT:
                    y = y_sum[:, k, :]
                    dve.wait_ge(fetched[k], 32 * (t // UN + 1))
                    link(dve.scalar_tensor_tensor(y, ya[:, k, 0, :], top_w[:, 0, t:t + 1], x2[:, t, :], ALU.mult, ALU.add))
                    link(dve.scalar_tensor_tensor(y, ya[:, k, 1, :], top_w[:, 1, t:t + 1], y, ALU.mult, ALU.add))
                    link(dve.bn_stats(stats[:, :], y))
                    dve.bn_aggr(mv[:, t % 2, :], stats[:, :]).then_inc(var_ready, 1)
                if t > 0:
                    y, s = y_sum[:, p, :], (t - 1) % 2
                    dve.wait_ge(std_ready, t)
                    dve.reciprocal(rstd[:, s:s + 1], std[:, s:s + 1]).then_inc(cv, 1)
                    n[0] += 1
                    link(dve.scalar_tensor_tensor(y, y, mv[:, s, 0:1], gam[:, :], ALU.subtract, ALU.mult))
                    link(dve.scalar_tensor_tensor(y, y, rstd[:, s:s + 1], bet[:, :], ALU.mult, ALU.add))
                    dve.wait_ge(x1_in[p], 16 * ((t - 1) // UN + 1))
                    if t - 1 >= UN:
                        dve.wait_ge(stored[p], 16 * ((t - 1) // UN))
                    dve.tensor_tensor(res[:, p, :], y, x1t[:, p, :], ALU.add).then_inc(done, 1)


_INS = ["x", "src", "dst", "edge_weight", "L0_gnn_W1", "L0_gnn_b1", "L0_gnn_ln_g1", "L0_gnn_ln_b1", "L0_gnn_W2",
        "L0_gnn_b2", "L0_gnn_ln_g2", "L0_gnn_ln_b2", "L0_ffn_gate_w", "L0_ffn_gate_b", "L0_ffn_w1", "L0_ffn_b1",
        "L0_ffn_w2", "L0_ffn_b2", "L0_ffn_gamma", "L0_ffn_beta"]


def kernel(**inputs):
    import numpy as _np
    import concourse.bacc as _bacc
    from concourse import mybir as _mybir
    from concourse.bass_utils import run_bass_kernel_spmd as _run

    nc = _bacc.Bacc("TRN2", target_bir_lowering=False, num_devices=1)
    arrays, args = {}, []
    for name in _INS:
        a = _np.ascontiguousarray(inputs[name])
        arrays[f"in_{name}_dram"] = a
        args.append(nc.dram_tensor(f"in_{name}_dram", a.shape, _mybir.dt.from_np(a.dtype), kind="ExternalInput").ap())
    args.append(nc.dram_tensor("out_0_dram", (N, D), _mybir.dt.float32, kind="ExternalOutput").ap())
    program(nc, *args)
    r = _run(nc, [arrays], core_ids=[0])
    return r.results[0]["out_0_dram"]
```

```python
from contextlib import ExitStack

import concourse.bass as bass
from concourse import mybir

F32 = mybir.dt.float32
BF16 = mybir.dt.bfloat16
I32 = mybir.dt.int32
U32 = mybir.dt.uint32
U16 = mybir.dt.uint16
ALU = mybir.AluOpType
ACT = mybir.ActivationFunctionType
AX_X = mybir.AxisListType.X

P = 128
N, D, E = 3125, 256, 50000
EXPERTS, F = 16, 512
EPS = 1e-5
KD, KF = D // P, F // P
NT = -(-N // P)
LAST = N - (NT - 1) * P
ET = -(-E // P)
EFULL = E // P
EREST = E - EFULL * P
EC = -(-ET // P)
GROUP = 8
RING = 2 * GROUP
STEPS = -(-(ET + NT - 1) // RING) * RING
BANKS, BANK = 8, 512
SLOTS, SLOT = 4, BANK
HOT = 4 * GROUP
ITERS = STEPS // RING
FLUSH = 3
UNITS = ITERS + NT
UN = 5
BLOCKS = (2 * N + EXPERTS * (P - 1)) // P
ROWS = BLOCKS * P
RARE = 6


def program(nc, x, src, dst, edge_weight, gw1, gb1, gg1, gn1, gw2, gb2, gg2, gn2,
            gate_w, gate_b, ew1, eb1, ew2, eb2, gamma, beta, out):
    tables = [nc.dram_tensor(f"scaled_rows{k}", ((NT + 1) * P, D), F32, kind="Internal").ap() for k in range(2)]
    x1_dram = nc.dram_tensor("after_gnn_plus_beta", ((NT + 1) * P, D), F32, kind="Internal").ap()
    rows_in = nc.dram_tensor("expert_rows_in", (ROWS, D), F32, kind="Internal").ap()
    rows_out = nc.dram_tensor("expert_rows_out", (ROWS, D), F32, kind="Internal").ap()

    with ExitStack() as outer:
        def sem(name):
            return outer.enter_context(nc.semaphore(name))

        def keep(name, shape, dt=F32):
            return outer.enter_context(nc.sbuf_tensor(name, shape, dt))

        ident = keep("ident", [P, P])
        eps = keep("eps", [P, 1])
        ones = keep("ones", [P, P], BF16)
        below = keep("below", [P, P], BF16)
        x2 = keep("x2", [P, NT + 1, D])
        slot_id = keep("slot_id", [P, 2, NT], I32)
        top_w = keep("top_w", [P, 2, NT])
        gwt = keep("gwt", [P, KD, EXPERTS])
        gbias = keep("gbias", [P, EXPERTS])
        logits = keep("logits", [P, NT, EXPERTS])
        used = keep("used", [P, 1], I32)
        w_off = keep("w_off", [P, BLOCKS], I32)
        ps = outer.enter_context(nc.psum_tensor("ps", [P, BANKS * BANK], F32))
        ps_slot = ps[:, :]
        ps_a, ps_b, ps_c, ps_d = (ps[:, k * BANK:(k + 1) * BANK] for k in range(4))

        zeroed_rows, zeroed_out = sem("zeroed_rows"), sem("zeroed_out")

        gnn(nc, sem, locals())
        w1 = keep("w1", [P, EXPERTS * KD * F])
        w2 = keep("w2", [P, EXPERTS * KF * D])
        w_in = sem("w_in")
        with ExitStack() as ctx:
            def sb(name, shape, dt=F32):
                return ctx.enter_context(nc.sbuf_tensor(name, shape, dt))
            gate(nc, sem, locals(), sb)
            route(nc, sem, locals(), logits, sb)
        experts(nc, sem, locals())


def gnn(nc, sem, g):
    x, src, dst, edge_weight = g["x"], g["src"], g["dst"], g["edge_weight"]
    ident, ones, below, x2 = g["ident"], g["ones"], g["below"], g["x2"]
    tables, x1_dram, rows_in = g["tables"], g["x1_dram"], g["rows_in"]
    ps_slot, ps_a, ps_b, ps_c, ps_d = g["ps_slot"], g["ps_a"], g["ps_b"], g["ps_c"], g["ps_d"]
    gwt, gbias, eps = g["gwt"], g["gbias"], g["eps"]
    with ExitStack() as ctx:
        def sb(name, shape, dt=F32):
            return ctx.enter_context(nc.sbuf_tensor(name, shape, dt))

        h = sb("h", [P, NT + 1, D])
        xin = sb("xin", [P, NT + 1, D])
        scaled = sb("scaled", [P, NT + 1, D])
        sums = sb("sums", [P, NT + 1, D])
        iota = sb("iota", [P, STEPS])
        node_next = sb("node_next", [P, STEPS], U16)
        slot_off = sb("slot_off", [P, STEPS], I32)
        ends = sb("ends", [P, 32], U16)
        rel = sb("rel", [P, STEPS])
        wgt = sb("wgt", [P, STEPS])
        src_i = sb("src_i", [P, STEPS], I32)
        zeros_b = sb("zeros_b", [P, D], BF16)
        zeros = sb("zeros", [P, 512])
        ones_f = sb("ones_f", [P, 1])
        deg = sb("deg", [P, NT])
        dis = sb("dis", [P, NT + 1])
        stats = sb("stats", [P, 6])
        mv = sb("mv", [P, NT, 2])
        rstd = sb("rstd", [P, NT])
        small = sb("small", [P, 8])
        wmat = sb("wmat", [P, 2, KD, D])
        beta = sb("beta_b", [P, D])
        vec = sb("vec", [P, 6, D])
        scratch = sb("scratch", [P, 8])

        unit_tile = sb("unit_tile", [P, UNITS + 1], I32)
        unit_wait = sb("unit_wait", [P, UNITS + 1], U16)
        left = sb("left", [P, 1], I32)

        setup_mem = ctx.enter_context(ExitStack())

        def tmp(name, shape, dt=F32):
            return setup_mem.enter_context(nc.sbuf_tensor(name, shape, dt))

        e_int = tmp("e_int", [P, 2, EC, P], I32)
        e_f = tmp("e_f", [P, 3, EC, P])
        bad_e = tmp("bad_e", [P, EC, P], I32)
        part = tmp("part", [P, EC])
        bounds = tmp("bounds", [P, NT])
        before = tmp("before", [P, EC, NT], BF16)
        first = tmp("first", [P, 1])
        begun = tmp("begun", [P, STEPS], BF16)
        node_of = tmp("node_of", [P, STEPS])
        edge_of = tmp("edge_of", [P, STEPS])
        pick = tmp("pick", [P, EC, STEPS])
        node_i = tmp("node_i", [P, STEPS], I32)
        ends_f = tmp("ends_f", [P, NT])
        valid = tmp("valid", [P, P])
        hot = tmp("hot", [P, HOT, P], BF16)
        iota_b = tmp("iota_b", [P, P], BF16)
        w_parts = tmp("w_parts", [P, STEPS, 4], BF16)
        w_rest = tmp("w_rest", [P, STEPS])
        deg_off = tmp("deg_off", [P, STEPS], I32)
        node_of4 = tmp("node_of4", [P, STEPS])
        w_group = tmp("w_group", [P, HOT // GROUP, GROUP, 4], BF16)
        rel_group = tmp("rel_group", [P, HOT // GROUP, GROUP])
        begun_units = tmp("begun_units", [P, UNITS + 1])
        complete = tmp("complete", [P, UNITS])
        plus_one = tmp("plus_one", [P, UNITS])
        unit_f = tmp("unit_f", [P, UNITS])
        taken = tmp("taken", [P, UNITS])
        shift0 = tmp("shift0", [P, NT])

        edges_in, x_in, small_in = sem("edges_in"), sem("x_in"), sem("small_in")
        consts, padded, spare = sem("consts"), sem("padded"), sem("spare")
        v = sem("vector_chain")
        var_ready, std_ready = sem("var_ready"), sem("std_ready")
        tiles_cmp, tiles_sum, first_ready, node_ps, pick_ready, step_ps = (
            sem(n) for n in ("tiles_cmp", "tiles_sum", "first_ready", "node_ps", "pick_ready", "step_ps"))

        with nc.Block() as block:
            @block.sync
            def _(sp):
                sp.wait_ge(padded, 4)
                for k, a in enumerate((dst, src)):
                    sp.dma_start(e_int[:, k, 0:EC - 1, :],
                                 a[0:(EC - 1) * P * P].rearrange("(c t p) -> t c p", t=P, p=P)).then_inc(edges_in, 16)
                    sp.dma_start(e_int[0:EFULL - (EC - 1) * P, k, EC - 1, :],
                                 a[(EC - 1) * P * P:EFULL * P].rearrange("(t p) -> t p", p=P)).then_inc(edges_in, 16)
                    sp.dma_start(e_int[EFULL - (EC - 1) * P:ET - (EC - 1) * P, k, EC - 1, 0:EREST],
                                 a[EFULL * P:E].rearrange("(t p) -> t p", t=1)).then_inc(edges_in, 16)
                a = edge_weight
                sp.dma_start(e_f[:, 2, 0:EC - 1, :],
                             a[0:(EC - 1) * P * P].rearrange("(c t p) -> t c p", t=P, p=P)).then_inc(edges_in, 16)
                sp.dma_start(e_f[0:EFULL - (EC - 1) * P, 2, EC - 1, :],
                             a[(EC - 1) * P * P:EFULL * P].rearrange("(t p) -> t p", p=P)).then_inc(edges_in, 16)
                sp.dma_start(e_f[EFULL - (EC - 1) * P:ET - (EC - 1) * P, 2, EC - 1, 0:EREST],
                             a[EFULL * P:E].rearrange("(t p) -> t p", t=1)).then_inc(edges_in, 16)
                sp.dma_start(xin[:, 0:NT - 1, :],
                             x[0:(NT - 1) * P, :].rearrange("(n p) d -> p n d", p=P)).then_inc(x_in, 16)
                sp.dma_start(xin[0:LAST, NT - 1, :], x[(NT - 1) * P:N, :]).then_inc(x_in, 16)
                for k, a in enumerate((g["gw1"], g["gw2"])):
                    sp.dma_start(wmat[:, k, :, :], a.rearrange("(k p) d -> p k d", p=P)).then_inc(small_in, 16)
                for k, name in enumerate(("gb1", "gg1", "gn1", "gb2", "gg2", "gn2")):
                    sp.dma_start(vec[:, k, :],
                                 g[name].rearrange("(a d) -> a d", a=1).to_broadcast([P, D])).then_inc(small_in, 16)
                sp.dma_start(beta[:, :], g["beta"].rearrange("(a d) -> a d", a=1).to_broadcast([P, D])).then_inc(small_in, 16)
                sp.dma_start(gwt[:, :, :], g["gate_w"].rearrange("(k p) e -> p k e", p=P)).then_inc(small_in, 16)
                sp.dma_start(gbias[:, :],
                             g["gate_b"].rearrange("(a d) -> a d", a=1).to_broadcast([P, EXPERTS])).then_inc(small_in, 16)
                sp.wait_ge(consts, 11)
                for k in range(ROWS // P // 2):
                    sp.dma_start(rows_in[2 * P * k:2 * P * (k + 1), :].rearrange("(p a) d -> p (a d)", a=2),
                                 zeros[:, :]).then_inc(g["zeroed_rows"], 16)
                for k in range(RARE // 2):
                    r = (BLOCKS - RARE + 2 * k) * P
                    sp.dma_start(g["rows_out"][r:r + 2 * P, :].rearrange("(p a) d -> p (a d)", a=2),
                                 zeros[:, :]).then_inc(g["zeroed_out"], 16)


            @block.gpsimd
            def _(pool):
                pool.memset(e_int[:, 0, EC - 1, :], 2 * NT * P).then_inc(padded, 1)
                pool.memset(e_int[:, 1, EC - 1, :], 0).then_inc(padded, 1)
                pool.memset(e_f[:, 2, EC - 1, :], 0.0).then_inc(padded, 1)
                pool.memset(xin[:, NT - 1, :], 0.0).then_inc(padded, 1)
                pool.memset(ident[:, :], 0.0).then_inc(consts, 1)
                pool.memset(ones[:, :], 1.0).then_inc(consts, 1)
                pool.memset(ones_f[:, :], 1.0).then_inc(consts, 1)
                pool.memset(eps[:, :], EPS).then_inc(consts, 1)
                pool.memset(below[:, :], 1.0).then_inc(consts, 1)
                pool.memset(valid[:, :], 1.0).then_inc(consts, 1)
                pool.memset(zeros[:, :], 0.0).then_inc(consts, 1)
                pool.memset(zeros_b[:, :], 0.0).then_inc(consts, 1)
                for a in (h, xin, scaled, sums):
                    pool.memset(a[:, NT, :], 0.0).then_inc(spare, 1)
                pool.memset(dis[:, NT:NT + 1], 0.0).then_inc(spare, 1)
                pool.memset(w_parts[:, :, 3:4], 0.0).then_inc(spare, 1)
                pool.memset(plus_one[:, :], 1.0).then_inc(spare, 1)
                pool.memset(complete[:, :], NT).then_inc(spare, 1)
                pool.memset(unit_tile[:, 0:1], NT).then_inc(spare, 1)
                pool.iota(iota[:, :], pattern=[[1, STEPS]], base=0, channel_multiplier=0,
                          allow_small_or_imprecise_dtypes=True).then_inc(consts, 1)
                pool.iota(part[:, :], pattern=[[P, EC]], base=0, channel_multiplier=1,
                          allow_small_or_imprecise_dtypes=True).then_inc(consts, 1)
                pool.iota(bounds[:, :], pattern=[[P, NT]], base=0, channel_multiplier=0,
                          allow_small_or_imprecise_dtypes=True).then_inc(consts, 1)
                pool.wait_ge(consts, 11)
                pool.affine_select(out=ident[:, :], in_=ident[:, :], compare_op=ALU.not_equal, fill=1.0,
                                   base=0, pattern=[[-1, P]], channel_multiplier=1).then_inc(consts, 1)
                pool.affine_select(out=below[:, :], in_=below[:, :], compare_op=ALU.is_gt, fill=0.0,
                                   base=0, pattern=[[1, P]], channel_multiplier=-1).then_inc(consts, 1)
                pool.affine_select(out=valid[:, :], in_=valid[:, :], compare_op=ALU.is_gt, fill=0.0,
                                   base=E - (EC - 1) * P * P, pattern=[[-1, P]], channel_multiplier=-P).then_inc(consts, 1)

            @block.vector
            def _(dve):
                n = [0]

                def link(ins):
                    n[0] += 1
                    ins.then_inc(v, 1)
                    dve.wait_ge(v, n[0])

                dve.wait_ge(consts, 14)
                dve.wait_ge(edges_in, 16 * 9)
                link(dve.tensor_copy(e_f[:, 0:2, :, :], e_int[:, :, :, :]))
                for c in range(EC):
                    ins = dve.tensor_scalar(before[:, c, :], bounds[:, :], e_f[:, 0, c, P - 1:P], None, ALU.is_gt)
                ins.then_inc(tiles_cmp, 1)
                ew = e_f[:, 2, :, :]
                link(dve.tensor_scalar(bad_e[:, :, :], ew, 0.0, 0.0, ALU.mult, ALU.not_equal))
                link(dve.copy_predicated(ew, bad_e[:, :, :], zeros[:, :].rearrange("p (c q) -> p c q", c=EC)))
                link(dve.scalar_tensor_tensor(ew, ew, -1.0, ew, ALU.mult, ALU.max))
                link(dve.tensor_scalar(ew, ew, 1e-6, None, ALU.max))
                link(dve.tensor_tensor(e_f[:, 2, EC - 1, :], e_f[:, 2, EC - 1, :], valid[:, :], ALU.mult))
                dve.wait_ge(tiles_sum, 1)
                link(dve.tensor_scalar(first[0:NT, :], ps_b[0:NT, 0:1], part[0:NT, 0:1], None, ALU.add))
                dve.tensor_scalar(begun[0:NT, :], iota[0:NT, :], first[0:NT, 0:1], None, ALU.is_ge).then_inc(first_ready, 1)
                link(dve.memset(ends_f[:, NT - 1:NT], STEPS))
                link(dve.tensor_tensor(ends_f[:, 0:NT - 1], ps_a[:, 1:NT], iota[:, 1:NT], ALU.add))
                link(dve.tensor_scalar(ends_f[:, :], ends_f[:, :], float(RING), None, ALU.add))
                link(dve.tensor_copy(ends[:, 0:NT], ends_f[:, :]))
                dve.wait_ge(node_ps, 1)
                link(dve.tensor_scalar(node_of[:, :], ps_c[:, 0:STEPS], 1.0, None, ALU.subtract))
                link(dve.tensor_tensor(edge_of[:, :], iota[:, :], node_of[:, :], ALU.subtract))
                for c in range(EC):
                    ins = dve.tensor_scalar(pick[:, c, :], edge_of[:, :], part[:, c:c + 1], None, ALU.is_equal)
                ins.then_inc(pick_ready, 1)
                link(dve.tensor_copy(node_i[:, :], node_of[:, :]))
                link(dve.tensor_scalar(slot_off[:, :], node_i[:, :], SLOTS - 1, 9, ALU.bitwise_and, ALU.logical_shift_left))
                link(dve.tensor_scalar(node_next[:, :], node_of[:, :], 1.0, None, ALU.add))
                link(dve.tensor_scalar(node_of4[:, :], node_of[:, :], 4.0, 7.0 * BANK, ALU.mult, ALU.add))
                link(dve.tensor_copy(deg_off[:, :], node_of4[:, :]))
                link(dve.tensor_copy(iota_b[:, :], iota[:, 0:P]))
                dve.wait_ge(spare, 9)
                link(dve.tensor_copy(complete[:, 0:ITERS], node_of[:, 0:STEPS:RING]))
                link(dve.memset(begun_units[:, 0:1], 0.0))
                link(dve.tensor_tensor_scan(begun_units[:, 1:UNITS + 1], plus_one[:, :], complete[:, :], 0.0, ALU.add, ALU.min))
                link(dve.tensor_tensor(taken[:, :], begun_units[:, 1:UNITS + 1], begun_units[:, 0:UNITS], ALU.subtract))
                link(dve.tensor_scalar(unit_f[:, :], begun_units[:, 0:UNITS], -float(NT), None, ALU.add))
                link(dve.tensor_tensor(unit_f[:, :], unit_f[:, :], taken[:, :], ALU.mult))
                link(dve.tensor_scalar(unit_tile[:, 1:UNITS + 1], unit_f[:, :], float(NT), None, ALU.add))
                link(dve.tensor_scalar(unit_wait[:, 0:UNITS], begun_units[:, 1:UNITS + 1], 1.0, None, ALU.add))
                link(dve.tensor_copy(left[:, :], begun_units[:, ITERS + FLUSH - 1:ITERS + FLUSH]))
                dve.wait_ge(x_in, 32)
                for t in range(NT):
                    link(dve.bn_stats(stats[:, :], xin[:, t, :]))
                    ins = dve.bn_aggr(mv[:, t, :], stats[:, :])
                    if t < NT - 1:
                        link(ins)
                ins.then_inc(var_ready, 1)
                dve.wait_ge(step_ps, 1)
                link(dve.scalar_tensor_tensor(rel[:, :], node_of[:, :], -float(P), ps_d[:, 0:STEPS], ALU.mult, ALU.add))
                dve.tensor_copy(src_i[:, :], ps_b[:, 0:STEPS])
                link(dve.tensor_copy(wgt[:, :], ps_a[:, 0:STEPS]))
                for k in range(3):
                    now = w_rest[:, :] if k else wgt[:, :]
                    link(dve.tensor_copy(w_parts[:, :, k:k + 1].rearrange("p s c -> p (s c)"), now))
                    if k < 2:
                        link(dve.tensor_tensor(w_rest[:, :], now, w_parts[:, :, k:k + 1].rearrange("p s c -> p (s c)"),
                                               ALU.subtract))
                dve.wait_ge(std_ready, 1)
                link(dve.reciprocal(rstd[:, :], rstd[:, :]))
                link(dve.scalar_tensor_tensor(shift0[:, :], mv[:, :, 0], -1.0, rstd[:, :], ALU.mult, ALU.mult))

            @block.scalar
            def _(act):
                act.wait_ge(var_ready, 1)
                act.activation(rstd[:, :], mv[:, :, 1], ACT.Sqrt, bias=eps[:, 0:1]).then_inc(std_ready, 1)

            @block.tensor
            def _(pe):
                pe.wait_ge(tiles_cmp, 1)
                for c in range(EC):
                    pe.matmul(ps_a[:, 0:NT], ones[:, :], before[:, c, :], start=(c == 0), stop=(c == EC - 1))
                for c in range(EC):
                    mm = pe.matmul(ps_b[0:NT, 0:1], before[:, c, :], ones[:, 0:1], start=(c == 0), stop=(c == EC - 1))
                mm.then_inc(tiles_sum, 1)
                pe.wait_ge(first_ready, 1)
                pe.matmul(ps_c[:, 0:STEPS], ones[0:NT, :], begun[0:NT, :], start=True, stop=True).then_inc(node_ps, 1)
                pe.wait_ge(pick_ready, 1)
                for k, ps in ((0, ps_d), (1, ps_b), (2, ps_a)):
                    for c in range(EC):
                        mm = pe.matmul(ps[:, 0:STEPS], e_f[:, k, c, :], pick[:, c, :], start=(c == 0), stop=(c == EC - 1))
                mm.then_inc(step_ps, 1)

        hot_free = sem("hot_free")
        hot_ready, deg_ps, deg_ready, dis_ready = (sem(n) for n in ("hot_ready", "deg_ps", "deg_ready", "dis_ready"))
        applied, marked, guarded = sem("applied"), sem("marked"), sem("guarded")
        dv, table_made, table_out = sem("deg_chain"), sem("table_made"), sem("table_out")
        ps_deg = ps_slot[:, 7 * BANK:7 * BANK + 4 * NT]
        ps_mark = [ps_slot[:, k * BANK:(k + 1) * BANK] for k in range(6)]
        assert STEPS % HOT == 0
        PAIRS = -(-NT // 2)
        with nc.Block() as block:
            @block.vector
            def _(dve):
                dve.memset(scratch[:, 0:1], 0.0).then_inc(hot_free, HOT)
                with dve.Fori(0, STEPS // HOT) as i:
                    dve.sem_clear(dv)
                    for g in range(HOT // GROUP):
                        dve.wait_ge(hot_free, i * HOT + (g + 1) * GROUP)
                        dve.tensor_tensor(w_group[:, g, :, :], w_parts[:, bass.ds(i * HOT + g * GROUP, GROUP), :],
                                          zeros_b[:, 0:4 * GROUP].rearrange("p (s c) -> p s c", c=4), ALU.add)
                        dve.tensor_tensor(rel_group[:, g, :], rel[:, bass.ds(i * HOT + g * GROUP, GROUP)],
                                          zeros[:, 0:GROUP], ALU.add).then_inc(dv, 1)
                        dve.wait_ge(dv, g + 1)
                        for k in range(GROUP):
                            ins = dve.tensor_scalar(hot[:, g * GROUP + k, :], iota_b[:, :], rel_group[:, g, k:k + 1], None,
                                                    ALU.is_equal)
                        ins.then_inc(hot_ready, 1)
                dve.sem_clear(dv)
                dve.wait_ge(deg_ps, 1)
                dve.tensor_reduce(deg[:, 0:NT], ps_deg.rearrange("p (n c) -> p n c", c=4), AX_X, ALU.add).then_inc(deg_ready, 1)
                for c in range(PAIRS):
                    w = min(2, NT - 2 * c) * D
                    dve.wait_ge(marked, c + 1)
                    dve.copy_predicated(h[:, 2 * c:2 * c + w // D, :].rearrange("p n d -> p (n d)"),
                                        ps_mark[c % len(ps_mark)][:, 0:w].bitcast(I32), zeros[:, 0:w]).then_inc(guarded, 1)
                    if c == 0:
                        dve.wait_ge(dis_ready, 1)
                        dve.reciprocal(dis[:, 0:NT], dis[:, 0:NT]).then_inc(dv, 1)

            @block.tensor
            def _(pe):
                pe.matmul(ps_deg, ones[:, :], zeros_b[:, 0:4 * NT], start=True, stop=False, skip_group_check=True)
                regs = [pe.alloc_register(f"deg_{k}") for k in range(GROUP)]
                with pe.Fori(0, STEPS // HOT) as i:
                    for k in range(HOT):
                        g, m = k // GROUP, k % GROUP
                        if m == 0:
                            pe.reg_load(regs, deg_off[0:1, bass.ds(i * HOT + k, GROUP)])
                            pe.wait_ge(hot_ready, i * (HOT // GROUP) + (g + 1))
                        off = pe.snap(regs[m], min_val=0, max_val=4 * NT - 4 + 7 * BANK)
                        mm = pe.matmul(ps_slot[:, bass.ds(off, 4)], hot[:, k, :], w_group[:, g, m, :],
                                       start=False, stop=False, skip_group_check=True)
                        if m == GROUP - 1:
                            mm.then_inc(hot_free, GROUP)
                pe.matmul(ps_slot[:, 6 * BANK:6 * BANK + 2], ones[:, :], zeros_b[:, 0:2], start=True, stop=True).then_inc(deg_ps, 1)

            @block.scalar
            def _(act):
                for t in range(NT):
                    act.activation(h[:, t, :], xin[:, t, :], ACT.Identity, bias=shift0[:, t:t + 1],
                                   scale=rstd[:, t:t + 1]).then_inc(applied, 1)

                def mark(c):
                    w = min(2, NT - 2 * c) * D
                    act.activation(ps_mark[c % len(ps_mark)][:, 0:w], h[:, 2 * c:2 * c + w // D, :].rearrange("p n d -> p (n d)"),
                                   ACT.Identity, bias=zeros[:, 0:1], scale=0.0).then_inc(marked, 1)

                act.wait_ge(applied, NT)
                for c in range(len(ps_mark)):
                    mark(c)
                act.wait_ge(deg_ready, 1)
                act.activation(dis[:, 0:NT], deg[:, :], ACT.Sqrt, bias=ones_f[:, 0:1]).then_inc(dis_ready, 1)
                act.wait_ge(dv, 1)
                for c in range(PAIRS):
                    act.wait_ge(guarded, c + 1)
                    for t in range(2 * c, min(NT, 2 * c + 2)):
                        act.activation(scaled[:, t, :], h[:, t, :], ACT.Copy, scale=dis[:, t:t + 1]).then_inc(table_made, 1)
                    if c + len(ps_mark) < PAIRS:
                        mark(c + len(ps_mark))

            @block.sync
            def _(sp):
                for c in range(NT // UN):
                    sp.wait_ge(table_made, UN * (c + 1))
                    sp.dma_start(tables[0][UN * P * c:UN * P * (c + 1), :].rearrange("(n p) d -> p n d", p=P),
                                 scaled[:, UN * c:UN * (c + 1), :]).then_inc(table_out, 16)
                sp.wait_ge(table_out, 16 * (NT // UN))
                sp.wait_ge(g["zeroed_out"], 16 * (RARE // 2))
                sp.wait_ge(small_in, 16 * 11)

        setup_mem.close()
        rows = sb("rows", [P, RING, D])
        smat = sb("smat", [P, RING, P])
        u = sb("u", [P, D])
        ut = sb("ut", [P, KD, P])
        y = sb("y", [P, D])
        z = sb("z", [P, D])
        x1s = sb("x1s", [P, D])
        x1b = sb("x1b", [P, D])
        ps_t, ps_y, ps_bad = (ps_slot[:, k * BANK:k * BANK + D] for k in (4, 5, 6))

        def layer_pass(q):
            bias, gain, shift = vec[:, 3 * q, :], vec[:, 3 * q + 1, :], vec[:, 3 * q + 2, :]
            ring_free, s_ready, slot_free, evac, u_ready, turned, ut_ready, y_ps, tile_done, stored, v = (
                sem(f"{n}_layer{q}") for n in ("ring_free", "s_ready", "slot_free", "evac", "u_ready", "turned", "ut_ready",
                                         "y_ps", "tile_done", "stored", "unit_chain"))
            landed = [sem(f"landed{q}_{k}") for k in range(RING)]
            target = x1_dram if q else tables[1]

            with nc.Block() as block:
                @block.gpsimd
                def _(pool):
                    for s in range(STEPS):
                        k = s % RING
                        if k % GROUP == 0 and s >= RING:
                            pool.wait_ge(ring_free, s + GROUP)
                        pool.indirect_dma_start(
                            rows[:, k, :], None, tables[q][0:NT * P, :],
                            bass.IndirectOffsetOnAxis(ap=src_i[:, s:s + 1].bitcast(U32), axis=0)).then_inc(landed[k], 16)

                @block.tensor
                def _(pe):
                    if q == 0:
                        for b in range(SLOTS):
                            mm = pe.matmul(ps_slot[:, SLOT * b:SLOT * b + D], ones[:, :], zeros_b[:, :],
                                           start=True, stop=False, skip_group_check=True)
                    pe.matmul(ps_y, ones[:, :], zeros_b[:, :], start=True, stop=True).then_inc(y_ps, 1)
                    regs = [pe.alloc_register(f"slot{q}_{k}") for k in range(GROUP)]
                    last = [pe.alloc_register(f"last{q}_{k}") for k in range(2)]

                    def steps(i, g):
                        pe.reg_load(regs, slot_off[0:1, bass.ds(i * RING + g * GROUP, GROUP)])
                        for k in range(2):
                            pe.reg_load(last[k], node_next[0:1, bass.ds(i * RING + (g * GROUP + SLOTS * (k + 1) - 1), 1)])
                        for k in range(GROUP):
                            if k % SLOTS == 0:
                                pe.wait_ge(slot_free, pe.snap(last[k // SLOTS], min_val=1, max_val=NT))
                            b = g * GROUP + k
                            pe.wait_ge(s_ready, i * RING + (b + 1))
                            pe.wait_ge(landed[b], i * 16 + 16)
                            off = pe.snap(regs[k], min_val=0, max_val=(SLOTS - 1) * SLOT)
                            pe.matmul(ps_slot[:, bass.ds(off, D)], smat[:, b, :], rows[:, b, :],
                                      start=False, stop=False, skip_group_check=True).then_inc(ring_free, 1)

                    def turn_u(i):
                        pe.wait_ge(u_ready, i + 1)
                        for c in range(KD):
                            mm = pe.transpose(ps_t[:, c * P:(c + 1) * P], u[:, c * P:(c + 1) * P], ident[:, :])
                        mm.then_inc(turned, 1)

                    def product(i):
                        pe.wait_ge(ut_ready, i + 1)
                        for c in range(KD):
                            mm = pe.matmul(ps_y, ut[:, c, :], wmat[:, q, c, :], start=(c == 0), stop=(c == KD - 1))
                        mm.then_inc(y_ps, 1)

                    with pe.Fori(0, ITERS) as i:
                        steps(i, 0)
                        turn_u(i)
                        steps(i, 1)
                        product(i)
                    with pe.Fori(ITERS, ITERS + FLUSH) as i:
                        turn_u(i)
                        product(i)
                    more = pe.alloc_register(f"more_pe{q}")
                    pe.reg_load(more, left[0:1, 0:1])
                    with pe.If(pe.snap(more, min_val=0, max_val=NT) < NT):
                        with pe.Fori(ITERS + FLUSH, UNITS) as i:
                            turn_u(i)
                            product(i)

                @block.scalar
                def _(act):
                    regs = [act.alloc_register(f"end{q}_{k}") for k in range(GROUP)]
                    for t in range(NT):
                        if t % GROUP == 0:
                            m = min(GROUP, NT - t)
                            act.reg_load(regs[0:m], ends[0:1, t:t + m])
                        s = (t % SLOTS) * SLOT
                        act.wait_ge(ring_free, act.snap(regs[t % GROUP], min_val=RING, max_val=RING + STEPS))
                        act.activation(sums[:, t, :], ps_slot[:, s:s + D], ACT.Copy).then_inc(evac, 1)
                        act.wait_ge(evac, t + 2)
                        act.activation(ps_slot[:, s:s + D], zeros[:, 0:D], ACT.Copy).then_inc(slot_free, 1)

                @block.vector
                def _(dve):
                    n = [0]

                    def link(ins):
                        n[0] += 1
                        ins.then_inc(v, 1)
                        dve.wait_ge(v, n[0])

                    def tile(a, t):
                        return a[:, bass.ds(t, 1), :].rearrange("p a d -> p (a d)")

                    def guard(a):
                        link(dve.tensor_scalar(ps_bad, a, 0.0, 0.0, ALU.mult, ALU.not_equal))
                        link(dve.copy_predicated(a, ps_bad.bitcast(I32), zeros[:, 0:D]))

                    def norm():
                        var, w, r, a, fin = (small[:, k:k + 1] for k in (1, 2, 3, 4, 5))
                        dve.tensor_scalar(fin, var, 3.0e38, None, ALU.is_le)
                        link(dve.tensor_scalar(w, var, EPS, 3.0e38, ALU.add, ALU.min))
                        link(dve.tensor_scalar(r.bitcast(I32), w.bitcast(I32), -0.5, 1597463007.0, ALU.mult, ALU.add))
                        for less in (3.0, 12.0, 768.0):
                            link(dve.scalar_tensor_tensor(a, r, w, r, ALU.mult, ALU.mult))
                            link(dve.scalar_tensor_tensor(r, a, less, r, ALU.subtract, ALU.mult))
                        link(dve.tensor_scalar(a, r, -1.0 / 8192.0, fin, ALU.mult, ALU.mult))
                        return a

                    def build(i, g):
                        dve.wait_ge(ring_free, i * RING + (g + 1) * GROUP)
                        for k in range(g * GROUP, (g + 1) * GROUP):
                            dve.tensor_scalar(smat[:, k, :], iota[:, 0:P], rel[:, bass.ds(i * RING + k, 1)],
                                              wgt[:, bass.ds(i * RING + k, 1)], ALU.is_equal, ALU.mult).then_inc(s_ready, 1)

                    unit_regs = [dve.alloc_register(f"unit{q}_{k}") for k in range(2)]
                    wait_reg = dve.alloc_register(f"unit_wait{q}")

                    def take_turned(i):
                        dve.wait_ge(turned, i + 1)
                        dve.tensor_copy(ut[:, :, :].rearrange("p c q -> p (c q)"), ps_t).then_inc(ut_ready, 1)

                    def unit(i, early):
                        dve.reg_load(unit_regs, unit_tile[0:1, bass.ds(i, 2)])
                        if not early:
                            dve.reg_load(wait_reg, unit_wait[0:1, bass.ds(i, 1)])
                        prev, cur = (dve.snap(r, min_val=0, max_val=NT) for r in unit_regs)
                        dve.sem_clear(v)
                        n[0] = 0
                        dve.wait_ge(y_ps, i + 1)
                        dve.scalar_tensor_tensor(y[:, :], ps_y, dis[:, bass.ds(prev, 1)], bias, ALU.mult, ALU.add).then_inc(v, 1)
                        n[0] += 1
                        if early:
                            dve.wait_ge(evac, NT + 1)
                            dve.wait_ge(tile_done, i)
                        else:
                            dve.wait_ge(evac, dve.snap(wait_reg, min_val=1, max_val=NT + 1))
                        dve.tensor_tensor(u[:, :], tile(sums, cur), tile(scaled, cur), ALU.add).then_inc(u_ready, 1)
                        dve.wait_ge(v, n[0])
                        guard(y[:, :])
                        link(dve.bn_stats(stats[:, :], y[:, :]))
                        link(dve.bn_aggr(small[:, 0:2], stats[:, :]))
                        if early:
                            take_turned(i)
                        r = norm()
                        link(dve.scalar_tensor_tensor(y[:, :], y[:, :], small[:, 0:1], gain, ALU.subtract, ALU.mult))
                        link(dve.scalar_tensor_tensor(y[:, :], y[:, :], r, shift, ALU.mult, ALU.add))
                        guard(y[:, :])
                        link(dve.scalar_tensor_tensor(z[:, :], y[:, :], 0.0, tile(h, prev), ALU.max, ALU.add))
                        guard(z[:, :])
                        dve.wait_ge(stored, i * 16 + 16)
                        if q == 0:
                            dve.tensor_scalar(tile(scaled, prev), z[:, :], dis[:, bass.ds(prev, 1)], None,
                                              ALU.mult).then_inc(tile_done, 1)
                            dve.tensor_copy(tile(h, prev), z[:, :])
                        else:
                            dve.tensor_tensor(x1s[:, :], z[:, :], tile(xin, prev), ALU.add).then_inc(v, 1)
                            n[0] += 1
                            dve.wait_ge(v, n[0])
                            dve.tensor_tensor(x1b[:, :], x1s[:, :], beta[:, :], ALU.add).then_inc(tile_done, 1)
                            link(dve.bn_stats(stats[:, :], x1s[:, :]))
                            link(dve.bn_aggr(small[:, 0:2], stats[:, :]))
                            r = norm()
                            dve.tensor_scalar(tile(x2, prev), x1s[:, :], small[:, 0:1], r, ALU.subtract, ALU.mult)
                        if not early:
                            take_turned(i)

                    for k, s in enumerate((ring_free, slot_free, evac, stored)):
                        dve.memset(scratch[:, k:k + 1], 0.0).then_inc(s, (RING, SLOTS, 1, 16)[k])
                    with dve.Fori(0, ITERS) as i:
                        build(i, 0)
                        build(i, 1)
                        unit(i, False)
                    with dve.Fori(ITERS, ITERS + FLUSH) as i:
                        unit(i, True)
                    more = dve.alloc_register(f"more_dve{q}")
                    dve.reg_load(more, left[0:1, 0:1])
                    with dve.If(dve.snap(more, min_val=0, max_val=NT) < NT):
                        with dve.Fori(ITERS + FLUSH, UNITS) as i:
                            unit(i, True)

                @block.sync
                def _(sp):
                    reg = sp.alloc_register(f"unit_sp{q}")

                    def store(i):
                        sp.reg_load(reg, unit_tile[0:1, bass.ds(i, 1)])
                        t = sp.snap(reg, min_val=0, max_val=NT)
                        sp.wait_ge(tile_done, i + 1)
                        sp.dma_start(target[bass.ds(t * P, P), :], x1b[:, :] if q else
                                     scaled[:, bass.ds(t, 1), :].rearrange("p a d -> p (a d)")).then_inc(stored, 16)

                    with sp.Fori(0, ITERS + FLUSH) as i:
                        store(i)
                    sp.wait_ge(stored, 16 * (ITERS + FLUSH + 1))
                    more = sp.alloc_register(f"more_sp{q}")
                    sp.reg_load(more, left[0:1, 0:1])
                    with sp.If(sp.snap(more, min_val=0, max_val=NT) < NT):
                        with sp.Fori(ITERS + FLUSH, UNITS) as i:
                            store(i)
                        sp.wait_ge(stored, 16 * (UNITS + 1))

        layer_pass(0)
        layer_pass(1)


def gate(nc, sem, g, sb):
    x2, ident, logits, ps_slot, gwt, gbias, w1, w2 = (
        g[n] for n in ("x2", "ident", "logits", "ps_slot", "gwt", "gbias", "w1", "w2"))
    x2_turned, x2t_ready, logit_ps, logits_out = (
        sem(n) for n in ("x2_turned", "x2t_ready", "logit_ps", "logits_out"))
    x2t = sb("x2t", [P, 2, KD, P])
    ps_x = [ps_slot[:, k * BANK:k * BANK + D] for k in range(2)]
    ps_l = [ps_slot[:, k * BANK:k * BANK + EXPERTS] for k in (2, 3)]
    with nc.Block() as block:
        @block.tensor
        def _(pe):
            def turn_x2(t):
                if t >= 2:
                    pe.wait_ge(x2t_ready, t - 1)
                for c in range(KD):
                    mm = pe.transpose(ps_x[t % 2][:, c * P:(c + 1) * P], x2[:, t, c * P:(c + 1) * P], ident[:, :])
                mm.then_inc(x2_turned, 1)

            turn_x2(0)
            for t in range(NT):
                if t + 1 < NT:
                    turn_x2(t + 1)
                pe.wait_ge(x2t_ready, t + 1)
                if t >= 2:
                    pe.wait_ge(logits_out, t - 1)
                for c in range(KD):
                    mm = pe.matmul(ps_l[t % 2], x2t[:, t % 2, c, :], gwt[:, c, :], start=(c == 0), stop=(c == KD - 1))
                mm.then_inc(logit_ps, 1)

        @block.scalar
        def _(act):
            for t in range(NT):
                act.wait_ge(x2_turned, t + 1)
                if t >= 2:
                    act.wait_ge(logit_ps, t - 1)
                act.activation(x2t[:, t % 2, :, :].rearrange("p c q -> p (c q)"), ps_x[t % 2], ACT.Copy).then_inc(x2t_ready, 1)

        @block.vector
        def _(dve):
            for t in range(NT):
                dve.wait_ge(logit_ps, t + 1)
                dve.tensor_tensor(logits[:, t, :], ps_l[t % 2], gbias[:, :], ALU.add).then_inc(logits_out, 1)

        @block.sync
        def _(sp):
            for e in range(EXPERTS):
                sp.dma_start(w1[:, e * KD * F:(e + 1) * KD * F].rearrange("p (k f) -> p k f", k=KD),
                             g["ew1"][e].rearrange("(k p) f -> p k f", p=P)).then_inc(g["w_in"], 16)
            for e in range(EXPERTS):
                sp.dma_start(w2[:, e * KF * D:(e + 1) * KF * D].rearrange("p (k f) -> p k f", k=KF),
                             g["ew2"][e].rearrange("(k p) f -> p k f", p=P)).then_inc(g["w_in"], 16)


def route(nc, sem, g, logits, sb):
    ones, below = g["ones"], g["below"]
    slot_id, top_w, w_off, ps_a, ps_b = g["slot_id"], g["top_w"], g["w_off"], g["ps_a"], g["ps_b"]
    one = [sb(f"one{k}", [P, NT, EXPERTS]) for k in range(2)]
    cand = sb("cand", [P, NT, EXPERTS])
    work = sb("work", [P, NT, EXPERTS])
    both = sb("both", [P, NT, EXPERTS], BF16)
    best = sb("best", [P, 2, NT])
    which = sb("which", [P, 2, NT])
    eids = sb("eids", [P, EXPERTS])
    live = sb("live", [P, NT])
    carry = sb("carry", [P, NT + 1, EXPERTS])
    count_i = sb("count_i", [P, EXPERTS], I32)
    nblk = sb("nblk", [P, 2, EXPERTS])
    blk_end = sb("blk_end", [P, EXPERTS])
    blk_start = sb("blk_start", [P, EXPERTS])
    bnum = sb("bnum", [P, BLOCKS])
    over = sb("over", [P, BLOCKS, EXPERTS])
    eid_b = sb("eid_b", [P, BLOCKS])
    slot_f = sb("slot_f", [P, 2, NT])
    gap = sb("gap", [P, NT])
    eg = sb("eg", [P, NT])
    neg = sb("neg", [P, NT, EXPERTS])
    flag = sb("flag", [P, NT, EXPERTS], I32)
    rc, ready, counted, v, ex = (sem(n) for n in ("route_consts", "route_onehot", "route_counted", "route_chain", "route_exp"))
    gapped = sem("route_gap")
    row = [P, NT, EXPERTS]

    def over_e(a):
        return a.rearrange("p (n e) -> p n e", e=1).to_broadcast(row)

    def over_n(a):
        return a.rearrange("p (n e) -> p n e", n=1).to_broadcast(row)

    with nc.Block() as block:
        @block.gpsimd
        def _(pool):
            pool.iota(eids[:, :], pattern=[[1, EXPERTS]], base=0, channel_multiplier=0,
                      allow_small_or_imprecise_dtypes=True).then_inc(rc, 1)
            pool.iota(bnum[:, :], pattern=[[1, BLOCKS]], base=0, channel_multiplier=0,
                      allow_small_or_imprecise_dtypes=True).then_inc(rc, 1)
            pool.memset(neg[:, :, :], -3.4e38).then_inc(rc, 1)
            pool.memset(live[:, :], 1.0).then_inc(rc, 1)
            pool.wait_ge(rc, 4)
            pool.affine_select(out=live[:, :], in_=live[:, :], compare_op=ALU.is_gt, fill=0.0, base=N,
                               pattern=[[-P, NT]], channel_multiplier=-1).then_inc(rc, 1)

        @block.tensor
        def _(pe):
            pe.wait_ge(ready, 1)
            both2 = both[:, :, :].rearrange("p n e -> p (n e)")
            pe.matmul(ps_a[:, 0:NT * EXPERTS], below[:, :], both2, start=True, stop=True)
            pe.matmul(ps_b[:, 0:NT * EXPERTS], ones[:, :], both2, start=True, stop=True).then_inc(counted, 1)

        @block.scalar
        def _(act):
            act.wait_ge(gapped, 1)
            act.activation(eg[:, :], gap[:, :], ACT.Exp).then_inc(ex, 1)

        @block.vector
        def _(dve):
            n = [0]

            def link(ins):
                n[0] += 1
                ins.then_inc(v, 1)
                dve.wait_ge(v, n[0])

            dve.wait_ge(rc, 5)
            for k in range(2):
                link(dve.tensor_reduce(best[:, k, :], logits[:, :, :], AX_X, ALU.max))
                link(dve.tensor_tensor(cand[:, :, :], logits[:, :, :], over_e(best[:, k, :]), ALU.is_equal))
                link(dve.tensor_scalar(cand[:, :, :], cand[:, :, :], -float(EXPERTS), float(EXPERTS), ALU.mult, ALU.add))
                link(dve.tensor_tensor(cand[:, :, :], cand[:, :, :], over_n(eids[:, :]), ALU.add))
                link(dve.tensor_reduce(which[:, k, :], cand[:, :, :], AX_X, ALU.min))
                link(dve.tensor_scalar(which[:, k, :], which[:, k, :], EXPERTS - 1.0, None, ALU.min))
                link(dve.tensor_tensor(one[k][:, :, :], over_n(eids[:, :]), over_e(which[:, k, :]), ALU.is_equal))
                if k == 0:
                    link(dve.tensor_copy(flag[:, :, :], one[0][:, :, :]))
                    link(dve.copy_predicated(logits[:, :, :], flag[:, :, :], neg[:, :, :]))
            dve.tensor_tensor(gap[:, :], best[:, 1, :], best[:, 0, :], ALU.subtract).then_inc(gapped, 1)
            link(dve.tensor_tensor(work[:, :, :], one[0][:, :, :], one[1][:, :, :], ALU.add))
            dve.tensor_tensor(both[:, :, :], work[:, :, :], over_e(live[:, :]), ALU.mult).then_inc(ready, 1)
            dve.wait_ge(ex, 1)
            link(dve.tensor_scalar(top_w[:, 0, :], eg[:, :], 1.0, None, ALU.add))
            link(dve.reciprocal(top_w[:, 0, :], top_w[:, 0, :]))
            link(dve.tensor_tensor(top_w[:, 1, :], top_w[:, 0, :], eg[:, :], ALU.mult))
            link(dve.memset(carry[:, 0, :], 0.0))
            dve.wait_ge(counted, 1)
            for t in range(NT):
                link(dve.tensor_tensor(carry[:, t + 1, :], carry[:, t, :], ps_b[:, t * EXPERTS:(t + 1) * EXPERTS], ALU.add))
            link(dve.tensor_scalar(nblk[:, 0, :], carry[:, NT, :], P - 1.0, None, ALU.add))
            link(dve.tensor_copy(count_i[:, :], nblk[:, 0, :]))
            link(dve.tensor_scalar(count_i[:, :], count_i[:, :], 7, None, ALU.logical_shift_right))
            link(dve.tensor_copy(nblk[:, 1, :], count_i[:, :]))
            link(dve.tensor_tensor_scan(blk_end[:, :], nblk[:, 1, :], carry[:, 0, :], 0.0, ALU.add, ALU.add))
            link(dve.tensor_copy(g["used"][:, :], blk_end[:, EXPERTS - 1:EXPERTS]))
            link(dve.tensor_tensor(blk_start[:, :], blk_end[:, :], nblk[:, 1, :], ALU.subtract))
            link(dve.tensor_scalar(blk_start[:, :], blk_start[:, :], float(P), None, ALU.mult))
            link(dve.tensor_tensor(work[:, :, :], carry[:, 0:NT, :],
                                   ps_a[:, 0:NT * EXPERTS].rearrange("p (n e) -> p n e", e=EXPERTS), ALU.add))
            link(dve.tensor_tensor(work[:, :, :], work[:, :, :], over_n(blk_start[:, :]), ALU.add))
            for k in range(2):
                link(dve.tensor_tensor(cand[:, :, :], work[:, :, :], one[k][:, :, :], ALU.mult))
                link(dve.tensor_reduce(slot_f[:, k, :], cand[:, :, :], AX_X, ALU.add))
            link(dve.tensor_copy(slot_id[:, :, :], slot_f[:, :, :]))
            wide = [P, BLOCKS, EXPERTS]
            link(dve.tensor_tensor(over[:, :, :], bnum[:, :].rearrange("p (b e) -> p b e", e=1).to_broadcast(wide),
                                   blk_end[:, :].rearrange("p (b e) -> p b e", b=1).to_broadcast(wide), ALU.is_ge))
            link(dve.tensor_reduce(eid_b[:, :], over[:, :, :], AX_X, ALU.add))
            link(dve.tensor_scalar(eid_b[:, :], eid_b[:, :], EXPERTS - 1.0, None, ALU.min))
            link(dve.tensor_copy(w_off[:, :], eid_b[:, :]))


def experts(nc, sem, g):
    used = g["used"]
    ident, x2, slot_id, top_w, w_off = g["ident"], g["x2"], g["slot_id"], g["top_w"], g["w_off"]
    rows_in, rows_out, x1_dram, out = g["rows_in"], g["rows_out"], g["x1_dram"], g["out"]
    ps_slot, ps_a, ps_b, ps_c, ps_d = g["ps_slot"], g["ps_a"], g["ps_b"], g["ps_c"], g["ps_d"]
    ring = 4
    usual = BLOCKS - RARE
    assert usual % ring == 2

    def more(eng, name):
        reg = eng.alloc_register(f"used_{name}")
        eng.reg_load(reg, used[0:1, 0:1])
        return eng.snap(reg, min_val=0, max_val=BLOCKS) > usual
    with ExitStack() as ctx:
        def sb(name, shape, dt=F32):
            return ctx.enter_context(nc.sbuf_tensor(name, shape, dt))

        with ExitStack() as inner:
            def sbi(name, shape, dt=F32):
                return inner.enter_context(nc.sbuf_tensor(name, shape, dt))
            w1, w2, w_in = g["w1"], g["w2"], g["w_in"]
            b1r = sbi("b1r", [EXPERTS * KF, P])
            b1t = sbi("b1t", [P, EXPERTS * KF])
            b2b = sbi("b2b", [P, EXPERTS * D])
            xb = sbi("xb", [P, ring, D])
            xt = sbi("xt", [P, 2, KD, P])
            w1s = sbi("w1s", [P, 2, KD, F])
            hidt = sbi("hidt", [P, 2, KF, P])
            yb = sbi("yb", [P, 2, D])
            unused = sbi("unused", [P, 2])
            unused_done = sem("unused_done")

            scattered, b_in = sem("scattered"), sem("b_in")
            b1_ps, b1_ready = sem("b1_ps"), sem("b1_ready")
            xb_in = [sem(f"xb_in{k}") for k in range(ring)]
            x_turned, xt_ready, w1_ready, h_ps, hidt_ready, out_ps, y_ready = (
                sem(n) for n in ("x_turned", "xt_ready", "w1_ready", "h_ps", "hidt_ready", "out_ps", "y_ready"))
            y_out = [sem(f"y_out{k}") for k in range(2)]
            with nc.Block() as block:
                @block.gpsimd
                def _(pool):
                    pool.wait_ge(g["zeroed_rows"], 16 * (ROWS // P // 2))
                    for t in range(NT):
                        m = P if t < NT - 1 else LAST
                        for k in range(2):
                            pool.indirect_dma_start(
                                rows_in[:, :], bass.IndirectOffsetOnAxis(ap=slot_id[0:m, k, t:t + 1].bitcast(U32), axis=0),
                                x2[0:m, t, :], None).then_inc(scattered, 16)
                    pool.wait_ge(scattered, 32 * NT)

                @block.sync
                def _(sp):
                    sp.dma_start(b1r[:, :], g["eb1"].rearrange("e (c p) -> (e c) p", p=P)).then_inc(b_in, 16)
                    sp.dma_start(b2b[:, :], g["eb2"].rearrange("(a e) d -> a (e d)", a=1).to_broadcast([P, EXPERTS * D])).then_inc(b_in, 16)
                    sp.wait_ge(scattered, 32 * NT)

                    def load(b, k):
                        sp.dma_start(xb[:, k, :], rows_in[bass.ds(b * P, P), :]).then_inc(xb_in[k], 16)

                    def store(b, k):
                        sp.wait_ge(y_ready, b + 3)
                        sp.dma_start(rows_out[bass.ds(b * P, P), :], yb[:, k % 2, :]).then_inc(y_out[k % 2], 16)

                    for k in range(ring):
                        load(k, k)
                    with sp.Fori(0, usual // ring) as i:
                        for k in range(ring):
                            sp.wait_ge(x_turned, i * ring + (k + 1))
                            load(i * ring + (k + ring), k)
                            store(i * ring + k, k)
                    for k in range(2):
                        store(usual - 2 + k, k)
                    for k in range(2):
                        sp.wait_ge(y_out[k], 16 * (usual // 2 + 1))
                    with sp.If(more(sp, "sp")):
                        for b in range(usual + 2, BLOCKS):
                            sp.wait_ge(x_turned, b - ring + 1)
                            load(b, b % ring)
                        for b in range(usual, BLOCKS):
                            store(b, b)
                        for k in range(2):
                            sp.wait_ge(y_out[k], 16 * (BLOCKS // 2 + 1))

                px, ph, py = ([ps_slot[:, (2 * j + k) * BANK:(2 * j + k) * BANK + w] for k in range(2)]
                              for j, w in enumerate((D, F, D)))
                pb = ps_slot[:, 0:EXPERTS * KF]

                @block.tensor
                def _(pe):
                    pe.wait_ge(b_in, 32)
                    pe.transpose(pb, b1r[:, :], ident[0:EXPERTS * KF, 0:EXPERTS * KF]).then_inc(b1_ps, 1)
                    pe.wait_ge(b1_ready, 1)
                    regs = [pe.alloc_register(f"expert{k}") for k in range(ring)]

                    def turn_x(b, q, loads):
                        pe.wait_ge(xb_in[q], loads * 16)
                        for c in range(KD):
                            mm = pe.transpose(px[q % 2][:, c * P:(c + 1) * P], xb[:, q, c * P:(c + 1) * P], ident[:, :])
                        mm.then_inc(x_turned, 1)

                    def up(b, s):
                        pe.wait_ge(w1_ready, b + 1)
                        pe.wait_ge(xt_ready, b + 1)
                        for f in range(KF):
                            for c in range(KD):
                                mm = pe.matmul(ph[s][:, f * P:(f + 1) * P], w1s[:, s, c, f * P:(f + 1) * P], xt[:, s, c, :],
                                               start=(c == 0), stop=(c == KD - 1))
                        mm.then_inc(h_ps, 1)

                    def down(b, s, e):
                        pe.wait_ge(hidt_ready, b + 1)
                        pe.wait_ge(y_ready, b + 1)
                        for c in range(KF):
                            mm = pe.matmul(py[s], hidt[:, s, c, :], w2[:, bass.ds(e * (KF * D) + c * D, D)],
                                           start=(c == 0), stop=(c == KF - 1))
                        mm.then_inc(out_ps, 1)

                    def expert(k):
                        return pe.snap(regs[k], min_val=0, max_val=EXPERTS - 1)

                    turn_x(0, 0, 1)
                    turn_x(1, 1, 1)
                    up(0, 0)
                    pe.wait_ge(w_in, 32 * EXPERTS)
                    pe.reg_load(regs[0:2], w_off[0:1, 0:2])
                    for b in range(2):
                        up(b + 1, (b + 1) % 2)
                        turn_x(b + 2, b + 2, 1)
                        down(b, b, expert(b))

                    def four_blocks(i):
                        pe.reg_load(regs, w_off[0:1, bass.ds(i * ring + 2, ring)])
                        for k in range(ring):
                            b = i * ring + (2 + k)
                            up(b + 1, (1 + k) % 2)
                            turn_x(b + 2, k, i + 2)
                            down(b, k % 2, expert(k))

                    with pe.Fori(0, usual // ring) as i:
                        four_blocks(i)
                    with pe.If(more(pe, "pe")):
                        with pe.Fori(usual // ring, BLOCKS // ring - 1) as i:
                            four_blocks(i)
                        pe.reg_load(regs[0:2], w_off[0:1, BLOCKS - 2:BLOCKS])
                        up(BLOCKS - 1, 1)
                        down(BLOCKS - 2, 0, expert(0))
                        down(BLOCKS - 1, 1, expert(1))

                @block.scalar
                def _(act):
                    act.wait_ge(b1_ps, 1)
                    act.activation(b1t[:, :], pb, ACT.Copy).then_inc(b1_ready, 1)
                    act.wait_ge(w_in, 32 * EXPERTS)
                    regs = [act.alloc_register(f"expert_a{k}") for k in range(2)]

                    def stage(k):
                        e = act.snap(regs[k], min_val=0, max_val=EXPERTS - 1)
                        act.activation(w1s[:, k, :, :].rearrange("p c f -> p (c f)"), w1[:, bass.ds(e * (KD * F), KD * F)],
                                       ACT.Copy).then_inc(w1_ready, 1)

                    def copy_x(b, s):
                        act.wait_ge(x_turned, b + 1)
                        act.activation(xt[:, s, :, :].rearrange("p c q -> p (c q)"), px[s], ACT.Copy).then_inc(xt_ready, 1)

                    act.reg_load(regs, w_off[0:1, 0:2])
                    for k in range(2):
                        stage(k)
                        copy_x(k, k)

                    def two_blocks(i):
                        act.reg_load(regs, w_off[0:1, bass.ds(i * 2 + 2, 2)])
                        for k in range(2):
                            act.wait_ge(h_ps, i * 2 + (k + 1))
                            act.activation(unused[:, k:k + 1], g["eps"][:, :], ACT.Copy).then_inc(unused_done, 1)
                            stage(k)
                            copy_x(i * 2 + (2 + k), k)

                    with act.Fori(0, usual // 2) as i:
                        two_blocks(i)
                    with act.If(more(act, "act")):
                        with act.Fori(usual // 2, BLOCKS // 2 - 1) as i:
                            two_blocks(i)

                @block.vector
                def _(dve):
                    dve.memset(yb[:, 0, 0:1], 0.0).then_inc(y_ready, 2)
                    dve.memset(yb[:, 0, 1:2], 0.0).then_inc(y_out[0], 16)
                    dve.memset(yb[:, 0, 2:3], 0.0).then_inc(y_out[1], 16)
                    dve.wait_ge(y_out[1], 16)
                    dve.wait_ge(b_in, 32)
                    dve.wait_ge(b1_ready, 1)
                    regs = [dve.alloc_register(f"expert_v{k}") for k in range(3)]

                    def relu_h(b, s, e):
                        dve.wait_ge(h_ps, b + 1)
                        for c in range(KF):
                            ins = dve.tensor_scalar(hidt[:, s, c, :], ph[s][:, c * P:(c + 1) * P],
                                                    b1t[:, bass.ds(e * KF + c, 1)], 0.0, ALU.add, ALU.max)
                        ins.then_inc(hidt_ready, 1)

                    def add_b2(b, s, e, uses):
                        dve.wait_ge(y_out[s], uses * 16)
                        dve.wait_ge(out_ps, b + 1)
                        dve.tensor_tensor(yb[:, s, :], py[s], b2b[:, bass.ds(e * D, D)], ALU.add).then_inc(y_ready, 1)

                    def expert(k):
                        return dve.snap(regs[k], min_val=0, max_val=EXPERTS - 1)

                    dve.reg_load(regs[0:2], w_off[0:1, 0:2])
                    relu_h(0, 0, expert(0))
                    relu_h(1, 1, expert(1))
                    add_b2(0, 0, expert(0), 1)
                    with dve.Fori(0, usual // 2 - 1) as i:
                        dve.reg_load(regs, w_off[0:1, bass.ds(i * 2 + 1, 3)])
                        for k in range(2):
                            relu_h(i * 2 + (2 + k), k, expert(k + 1))
                            add_b2(i * 2 + (1 + k), (1 + k) % 2, expert(k), i + (1 + k))
                    dve.reg_load(regs[0:1], w_off[0:1, usual - 1:usual])
                    add_b2(usual - 1, 1, expert(0), usual // 2)
                    with dve.If(more(dve, "dve")):
                        for b in range(usual, BLOCKS):
                            dve.reg_load(regs[0:1], w_off[0:1, b:b + 1])
                            relu_h(b, b % 2, expert(0))
                            add_b2(b, b % 2, expert(0), b // 2 + 1)

        combine(nc, sem, g, sb)


def combine(nc, sem, g, sb):
    x2, slot_id, top_w, rows_out, x1_dram, out = (g[n] for n in ("x2", "slot_id", "top_w", "rows_out", "x1_dram", "out"))
    ya = sb("ya", [P, UN, 2, D])
    x1t = sb("x1t", [P, UN, D])
    y_sum = sb("y_sum", [P, UN, D])
    res = sb("res", [P, UN, D])
    gam = sb("gam", [P, D])
    stats = sb("stats2", [P, 6])
    mv = sb("mv2", [P, 2, 2])
    std = sb("std2", [P, 2])
    rstd = sb("rstd2", [P, 2])
    fetched = [sem(f"fetched{k}") for k in range(UN)]
    x1_in = [sem(f"x1_in{k}") for k in range(UN)]
    stored = [sem(f"stored{k}") for k in range(UN)]
    var_ready, std_ready = sem("var_ready2"), sem("std_ready2")
    padded, gb_in, cv, done = sem("padded2"), sem("gb_in"), sem("combine_chain"), sem("combined")
    with nc.Block() as block:
        @block.gpsimd
        def _(pool):
            pool.memset(ya[:, UN - 1, :, :], 0.0).then_inc(padded, 1)
            pool.wait_ge(padded, 1)
            for t in range(NT):
                m = P if t < NT - 1 else LAST
                if t >= UN:
                    pool.wait_ge(done, t - UN + 1)
                for k in range(2):
                    pool.indirect_dma_start(
                        ya[0:m, t % UN, k, :], None, rows_out[:, :],
                        bass.IndirectOffsetOnAxis(ap=slot_id[0:m, k, t:t + 1].bitcast(U32), axis=0)
                    ).then_inc(fetched[t % UN], 16)

        @block.sync
        def _(sp):
            sp.dma_start(gam[:, :], g["gamma"].rearrange("(a d) -> a d", a=1).to_broadcast([P, D])).then_inc(gb_in, 16)
            for t in range(NT + UN - 1):
                if t < NT:
                    if t >= UN:
                        sp.wait_ge(done, t - UN + 1)
                    sp.dma_start(x1t[:, t % UN, :], x1_dram[t * P:(t + 1) * P, :]).then_inc(x1_in[t % UN], 16)
                d = t - (UN - 1)
                if d >= 0:
                    m = P if d < NT - 1 else LAST
                    sp.wait_ge(done, d + 1)
                    sp.dma_start(out[d * P:d * P + m, :], res[0:m, d % UN, :]).then_inc(stored[d % UN], 16)
            for k in range(UN):
                sp.wait_ge(stored[k], 16 * (NT // UN))

        @block.scalar
        def _(act):
            for t in range(NT):
                act.wait_ge(var_ready, t + 1)
                act.activation(std[:, t % 2:t % 2 + 1], mv[:, t % 2, 1:2], ACT.Sqrt, bias=g["eps"][:, 0:1]).then_inc(std_ready, 1)

        @block.vector
        def _(dve):
            dve.wait_ge(gb_in, 16)
            n = [0]

            def link(ins):
                n[0] += 1
                ins.then_inc(cv, 1)
                dve.wait_ge(cv, n[0])

            for t in range(NT + 1):
                k, p = t % UN, (t - 1) % UN
                if t < NT:
                    y = y_sum[:, k, :]
                    dve.wait_ge(fetched[k], 32 * (t // UN + 1))
                    link(dve.scalar_tensor_tensor(y, ya[:, k, 0, :], top_w[:, 0, t:t + 1], x2[:, t, :], ALU.mult, ALU.add))
                    link(dve.scalar_tensor_tensor(y, ya[:, k, 1, :], top_w[:, 1, t:t + 1], y, ALU.mult, ALU.add))
                    link(dve.bn_stats(stats[:, :], y))
                    dve.bn_aggr(mv[:, t % 2, :], stats[:, :]).then_inc(var_ready, 1)
                if t > 0:
                    y, s = y_sum[:, p, :], (t - 1) % 2
                    dve.wait_ge(std_ready, t)
                    dve.reciprocal(rstd[:, s:s + 1], std[:, s:s + 1]).then_inc(cv, 1)
                    n[0] += 1
                    link(dve.scalar_tensor_tensor(y, y, mv[:, s, 0:1], gam[:, :], ALU.subtract, ALU.mult))
                    dve.wait_ge(x1_in[p], 16 * ((t - 1) // UN + 1))
                    if t - 1 >= UN:
                        dve.wait_ge(stored[p], 16 * ((t - 1) // UN))
                    dve.scalar_tensor_tensor(res[:, p, :], y, rstd[:, s:s + 1], x1t[:, p, :], ALU.mult, ALU.add).then_inc(done, 1)


_INS = ["x", "src", "dst", "edge_weight", "L0_gnn_W1", "L0_gnn_b1", "L0_gnn_ln_g1", "L0_gnn_ln_b1", "L0_gnn_W2",
        "L0_gnn_b2", "L0_gnn_ln_g2", "L0_gnn_ln_b2", "L0_ffn_gate_w", "L0_ffn_gate_b", "L0_ffn_w1", "L0_ffn_b1",
        "L0_ffn_w2", "L0_ffn_b2", "L0_ffn_gamma", "L0_ffn_beta"]


def kernel(**inputs):
    import numpy as _np
    import concourse.bacc as _bacc
    from concourse import mybir as _mybir
    from concourse.bass_utils import run_bass_kernel_spmd as _run

    nc = _bacc.Bacc("TRN2", target_bir_lowering=False, num_devices=1)
    arrays, args = {}, []
    for name in _INS:
        a = _np.ascontiguousarray(inputs[name])
        arrays[f"in_{name}_dram"] = a
        args.append(nc.dram_tensor(f"in_{name}_dram", a.shape, _mybir.dt.from_np(a.dtype), kind="ExternalInput").ap())
    args.append(nc.dram_tensor("out_0_dram", (N, D), _mybir.dt.float32, kind="ExternalOutput").ap())
    program(nc, *args)
    r = _run(nc, [arrays], core_ids=[0])
    return r.results[0]["out_0_dram"]
```
